# Optimizing a Trainium2 kernel written in Bass

```python
import numpy as np
import jax
import jax.numpy as jnp

def _softmax(x, axis=-1):
    return jax.nn.softmax(x, axis=axis)

def _gelu(x):
    return jax.nn.gelu(x, approximate=True)

def _silu(x):
    return jax.nn.silu(x)

def _sigmoid(x):
    return jax.nn.sigmoid(x)

def _layernorm(x, axis=-1, eps=1e-05):
    m = jnp.mean(x, axis=axis, keepdims=True)
    v = jnp.var(x, axis=axis, keepdims=True)
    return (x - m) / jnp.sqrt(v + eps)

def _scatter_add(tgt, idx, src, axis=0):
    return tgt.at[idx].add(src)

def _segment_sum(src, seg, n):
    return jax.ops.segment_sum(src, seg, n)
kernel_name = 'mk_macaron_d1_jaxref_r8_ef791e'

def setup_inputs(seed: int=0):
    np.random.seed(seed)
    _w = jnp.asarray

    def _L0_attn_setup():
        import jax, jax.numpy as jnp
        import numpy as np
        B, S, D = (4, 256, 128)
        H = 16
        HS = D // H
        SCALE = HS ** 0.5
        key = jax.random.key(seed)
        ks = jax.random.split(key, 9)
        std = 1.0 / np.sqrt(D)

        def lin(kw, kb, fan_in, fan_out):
            w = jax.random.uniform(kw, (fan_in, fan_out), minval=-std, maxval=std, dtype=jnp.float32)
            b = jax.random.uniform(kb, (fan_out,), minval=-std, maxval=std, dtype=jnp.float32)
            return (w, b)
        Wq, bq = lin(ks[0], ks[1], D, D)
        Wk, bk = lin(ks[2], ks[3], D, D)
        Wv, bv = lin(ks[4], ks[5], D, D)
        Wm, bm = lin(ks[6], ks[7], D, D)
        x = jax.random.normal(ks[8], (B, S, D), dtype=jnp.float32)
        return {'x': x, 'Wq': Wq, 'bq': bq, 'Wk': Wk, 'bk': bk, 'Wv': Wv, 'bv': bv, 'Wm': Wm, 'bm': bm}
    _L0_attn_in = _L0_attn_setup()

    def _L0_ffn_setup():
        import jax, jax.numpy as jnp
        import numpy as np
        DIM = 128
        MOE_HID = 64
        SHARED_HID = 256
        N_EXPERTS = 16
        TOP_K = 2
        NORM_TOPK_PROB = True
        key = jax.random.key(seed)
        ks = jax.random.split(key, 9)
        s = 0.02
        x = jax.random.normal(ks[0], (2, 128, DIM), dtype=jnp.float32)
        Wg = jax.random.normal(ks[1], (N_EXPERTS, DIM), dtype=jnp.float32) * s
        We_gate = jax.random.normal(ks[2], (N_EXPERTS, MOE_HID, DIM), dtype=jnp.float32) * s
        We_up = jax.random.normal(ks[3], (N_EXPERTS, MOE_HID, DIM), dtype=jnp.float32) * s
        We_down = jax.random.normal(ks[4], (N_EXPERTS, DIM, MOE_HID), dtype=jnp.float32) * s
        Ws_gate = jax.random.normal(ks[5], (SHARED_HID, DIM), dtype=jnp.float32) * s
        Ws_up = jax.random.normal(ks[6], (SHARED_HID, DIM), dtype=jnp.float32) * s
        Ws_down = jax.random.normal(ks[7], (DIM, SHARED_HID), dtype=jnp.float32) * s
        Wsg = jax.random.normal(ks[8], (1, DIM), dtype=jnp.float32) * s
        return {'x': x, 'Wg': Wg, 'We_gate': We_gate, 'We_up': We_up, 'We_down': We_down, 'Ws_gate': Ws_gate, 'Ws_up': Ws_up, 'Ws_down': Ws_down, 'Wsg': Wsg}
    _L0_ffn_in = _L0_ffn_setup()
    _d = {'L0_attn_x': _L0_attn_in['x'], 'L0_attn_Wq': _L0_attn_in['Wq'], 'L0_attn_bq': _L0_attn_in['bq'], 'L0_attn_Wk': _L0_attn_in['Wk'], 'L0_attn_bk': _L0_attn_in['bk'], 'L0_attn_Wv': _L0_attn_in['Wv'], 'L0_attn_bv': _L0_attn_in['bv'], 'L0_attn_Wm': _L0_attn_in['Wm'], 'L0_attn_bm': _L0_attn_in['bm'], 'L0_ffn_Wg': _L0_ffn_in['Wg'], 'L0_ffn_We_gate': _L0_ffn_in['We_gate'], 'L0_ffn_We_up': _L0_ffn_in['We_up'], 'L0_ffn_We_down': _L0_ffn_in['We_down'], 'L0_ffn_Ws_gate': _L0_ffn_in['Ws_gate'], 'L0_ffn_Ws_up': _L0_ffn_in['Ws_up'], 'L0_ffn_Ws_down': _L0_ffn_in['Ws_down'], 'L0_ffn_Wsg': _L0_ffn_in['Wsg']}
    _x0 = _d['L0_attn_x']
    _d['L0_attn_x'] = jax.random.normal(jax.random.fold_in(jax.random.key(seed), 1), (2, 1024, 128), dtype=_x0.dtype)
    del _x0
    return _d

def reference(L0_attn_x, L0_attn_Wq, L0_attn_bq, L0_attn_Wk, L0_attn_bk, L0_attn_Wv, L0_attn_bv, L0_attn_Wm, L0_attn_bm, L0_ffn_Wg, L0_ffn_We_gate, L0_ffn_We_up, L0_ffn_We_down, L0_ffn_Ws_gate, L0_ffn_Ws_up, L0_ffn_Ws_down, L0_ffn_Wsg):

    def _L0_attn_ref(x, Wq, bq, Wk, bk, Wv, bv, Wm, bm):
        import jax, jax.numpy as jnp
        import numpy as np
        B, S, D = (4, 256, 128)
        H = 16
        HS = D // H
        SCALE = HS ** 0.5
        bs, seq, _ = x.shape

        def heads(w, b):
            return (x @ w + b).reshape(bs, seq, H, HS).transpose(0, 2, 1, 3)
        q = heads(Wq, bq)
        k = heads(Wk, bk)
        v = heads(Wv, bv)
        scores = jnp.einsum('bhqd,bhkd->bhqk', q, k) / SCALE
        causal_mask = jnp.arange(seq)[None, :] > jnp.arange(seq)[:, None]
        scores = jnp.where(causal_mask, jnp.float32(-1000000000000.0), scores)
        probs = jax.nn.softmax(scores, axis=-1)
        attn = jnp.einsum('bhqk,bhkd->bhqd', probs, v)
        attn = attn.transpose(0, 2, 1, 3).reshape(bs, seq, H * HS)
        return attn @ Wm + bm

    def _L0_ffn_ref(x, Wg, We_gate, We_up, We_down, Ws_gate, Ws_up, Ws_down, Wsg):
        import jax, jax.numpy as jnp
        import numpy as np
        DIM = 128
        MOE_HID = 64
        SHARED_HID = 256
        N_EXPERTS = 16
        TOP_K = 2
        NORM_TOPK_PROB = True
        B, S, D = x.shape
        xt = x.reshape(-1, D)
        gates = jax.nn.softmax(xt @ Wg.T, axis=-1)
        scores, inds = jax.lax.top_k(gates, TOP_K)
        if NORM_TOPK_PROB:
            scores = scores / jnp.sum(scores, axis=-1, keepdims=True)
        g = jnp.einsum('td,ehd->teh', xt, We_gate)
        u = jnp.einsum('td,ehd->teh', xt, We_up)
        h = jax.nn.silu(g) * u
        y_all = jnp.einsum('teh,edh->ted', h, We_down)
        y_sel = jnp.take_along_axis(y_all, inds[:, :, None], axis=1)
        y = jnp.sum(y_sel * scores[:, :, None], axis=1)
        shared = jax.nn.silu(xt @ Ws_gate.T) * (xt @ Ws_up.T) @ Ws_down.T
        y = y + jax.nn.sigmoid(xt @ Wsg.T) * shared
        return y.reshape(B, S, D)
    x = L0_attn_x
    x = x + 0.5 * _L0_ffn_ref(_layernorm(x, axis=-1), L0_ffn_Wg, L0_ffn_We_gate, L0_ffn_We_up, L0_ffn_We_down, L0_ffn_Ws_gate, L0_ffn_Ws_up, L0_ffn_Ws_down, L0_ffn_Wsg)
    x = x + _L0_attn_ref(_layernorm(x, axis=-1), L0_attn_Wq, L0_attn_bq, L0_attn_Wk, L0_attn_bk, L0_attn_Wv, L0_attn_bv, L0_attn_Wm, L0_attn_bm)
    x = x + 0.5 * _L0_ffn_ref(_layernorm(x, axis=-1), L0_ffn_Wg, L0_ffn_We_gate, L0_ffn_We_up, L0_ffn_We_down, L0_ffn_Ws_gate, L0_ffn_Ws_up, L0_ffn_Ws_down, L0_ffn_Wsg)
    return x

_drawn_inputs = setup_inputs


def setup_inputs(seed=0):
    import zlib

    import numpy as np

    out = dict(_drawn_inputs(seed))
    spreads = {}
    factors = {'L0_attn_Wq': 4.286,
     'L0_attn_bq': 8.0,
     'L0_attn_Wk': 4.276,
     'L0_attn_bk': 8.0,
     'L0_ffn_Wg': 8.0,
     'L0_ffn_We_gate': 8.0,
     'L0_ffn_We_up': 8.0,
     'L0_ffn_We_down': 8.0,
     'L0_ffn_Ws_gate': 8.0,
     'L0_ffn_Ws_up': 8.0,
     'L0_ffn_Ws_down': 8.0,
     'L0_ffn_Wsg': 8.0}
    for name, (base, spread) in spreads.items():
        noise = np.random.default_rng([zlib.crc32(name.encode()), seed]).standard_normal(out[name].shape)
        drawn = base * np.exp(spread * noise) if base else spread * noise
        out[name] = jnp.asarray(drawn.astype(out[name].dtype))
    for name, factor in factors.items():
        out[name] = (out[name] * factor).astype(out[name].dtype)
    return out
```

```python
import concourse.bass as bass
from concourse import mybir
from contextlib import ExitStack

F32 = mybir.dt.float32
BF16 = mybir.dt.bfloat16
U32 = mybir.dt.uint32
ALU = mybir.AluOpType
ACT = mybir.ActivationFunctionType
AX = mybir.AxisListType

P = 128
D = 128
B, S = 2, 1024
T = B * S
NT = T // P
CH = 512
TC = CH // P
NCH = T // CH
E, MH, SH = 16, 64, 256
EH = E * MH + SH
NF = EH // P
NR = E + 1
H, HS = 16, 8
SCALE = HS ** -0.5
NQ = 4
HQ = H // NQ
TB = S // P
CB = S // CH
ROWS = 9 * HS
SHIFT = ROWS
VC = 32
EPS = 1e-5
BIG = -1e30

HALF0 = [(0, h, i, 0) for i in range(TC) for h in range(HQ)]
HALF1 = [(1, h, i, p) for i in range(TC) for h in range(HQ) for p in range(2)]
TURNS = HALF0 + HALF1[:2] + ["max0"] + HALF1[2:] + ["max1"]
NTURN = len(TURNS)
LAST_MAX0 = 16
LAST_MAX1 = NTURN - 1
UNITS = [(cc, j) for cc in range(CB) for j in range(TC * (cc + 1))]
NU = len(UNITS)
NPB = 3


def unit_shape(cc, j):
    q0 = max(CH * cc, P * j)
    return q0, CH * (cc + 1) - q0, P * j >= CH * cc


def macaron(nc, x_in, w_gate, w_up, w_down, w_route, Wq, bq, Wk, bk, Wv, bv, Wm, bm, out):
    ctx = ExitStack()
    with ctx:
        def sb(name, shape, dt=F32):
            return ctx.enter_context(nc.sbuf_tensor(name, shape, dt))

        def sem(name):
            return ctx.enter_context(nc.semaphore(name))

        x = sb("x", [P, NT, D])
        wg = sb("wg", [P, NF, P])
        wu = sb("wu", [P, NF, P])
        wd = sb("wd", [P, NF, D])
        wr = sb("wr", [P, NR])
        wq = sb("wq", [P, P])
        wk = sb("wk", [P, P])
        wv = sb("wv", [P, P])
        wm = sb("wm", [P, P])
        bqk = sb("bqk", [P, 2])
        bqs = sb("bqs", [P, 1])
        bvb = sb("bvb", [P, P])
        bmr = sb("bmr", [1, P])
        ones_row = sb("ones_row", [1, P])
        ident = sb("ident", [P, P])
        identb = sb("identb", [P, P], BF16)
        sel = sb("sel", [3 * NR, NF, P], BF16)
        iota_e = sb("iota_e", [P, E])
        neg_half = sb("neg_half", [P, TC])
        mask = sb("mask", [P, CH])
        st = sb("st", [P, TC, 6])
        mv = sb("mv", [P, TC, 2])
        ve = sb("ve", [P, TC])
        rstd = sb("rstd", [P, TC])
        xn = sb("xn", [P, TC, D])
        xT = sb("xT", [P, NCH, CH])
        xTa = xT[:, 0:CB, :]
        lgT = sb("lgT", [NR, CH])
        lg = sb("lg", [P, TC, NR])
        mx8 = sb("mx8", [P, TC, 8])
        ix8 = sb("ix8", [P, TC, 8], U32)
        ixf = sb("ixf", [P, TC, 2])
        dz = sb("dz", [P, 2, TC])
        th = sb("th", [P, 2, TC])
        rw = sb("rw", [P, 3, TC])
        e1 = sb("e1", [P, TC, E])
        e2 = sb("e2", [P, TC, E])
        cf = sb("cf", [P, TC, NR])
        cr = sb("cr", [P, TC, NR])
        cp = sb("cp", [P, TC, 3, NR], BF16)
        cT = sb("cT", [3 * NR, NCH, CH], BF16)
        sg = sb("sg", [P, 2, CH])
        su = sb("su", [P, 2, CH])
        hh = sb("hh", [P, 2, CH])
        yT = sb("yT", [P, CH])
        qf = sb("qf", [P, 2, CH])
        qr = sb("qr", [P, 2, CH])
        qp = sb("qp", [P, 2, 3, CH], BF16)
        Qs = sb("Qs", [P, NQ, HQ, S], BF16)
        Ks = sb("Ks", [P, NQ, HQ, S], BF16)
        zrow = sb("zrow", [2, S], BF16)
        Vs = sb("Vs", [P, TB, H, VC])
        junk = sb("junk", [P, 2, CH], BF16)
        mmx = sb("mmx", [P, 2, 2, HQ, TC])
        m2 = sb("m2", [P, 2, HQ, TC, 2])
        srow = sb("srow", [HQ * TC, 2, 2, P], BF16)
        pr = sb("pr", [P, NPB, HQ, CH])
        oT = sb("oT", [P, NQ, S])
        rec = sb("rec", [P, 2, H])
        at = sb("at", [P, 2, P])
        atT = sb("atT", [P, 2, P])

        ps = ctx.enter_context(nc.psum_tensor("ps", [P, 8, CH], F32))
        parts = nc.dram_tensor("parts", [2, 3, P, T], BF16, kind="Internal").ap()
        out_v = out.rearrange("(n p) d -> p n d", p=P)

        x_first_loaded = sem("x_first_loaded")
        x_rest_loaded = sem("x_rest_loaded")
        ffn_w_loaded = sem("ffn_w_loaded")
        attn_w_loaded = sem("attn_w_loaded")
        const_step = sem("const_step")
        const_done = sem("const_done")
        pads_done = sem("pads_done")
        vstep = sem("vstep")
        out_stored = sem("out_stored")
        FFN_SEMS = ("ve_ready", "pow_done", "xn_ready", "xT_psum", "xT_ready", "lgT_psum", "lgT_ready",
                    "lg_psum", "lg_read", "dz_ready", "th_ready", "cp_ready", "cT_psum", "cT_ready",
                    "g_psum", "uc_psum", "sg_ready", "su_done", "h_ready", "h_used",
                    "yT_ready", "yb_psum", "y_added")
        ffn_sems = [{n: sem(f"{n}{k}") for n in FFN_SEMS} for k in range(2)]
        bqs_ready = sem("bqs_ready")
        aq_ve, aq_pow, aq_xn = sem("aq_ve"), sem("aq_pow"), sem("aq_xn")
        aq_xT_psum, aq_xT = sem("aq_xT_psum"), sem("aq_xT")
        qk_psum, v_psum = sem("qk_psum"), sem("v_psum")
        part0_ready, rest_ready = sem("part0_ready"), sem("rest_ready")
        part1_ready, part2_ready = sem("part1_ready"), sem("part2_ready")
        v_ready = sem("v_ready")
        parts_stored = sem("parts_stored")
        stack_loaded = [sem(f"stack_loaded{n}") for n in range(NQ)]
        shift_loaded = [sem(f"shift_loaded{h}") for h in range(2)]
        a_psum, a_done, max1_ready = sem("a_psum"), sem("a_done"), sem("max1_ready")
        st_psum, exp_done, p_masked, pv_done = sem("st_psum"), sem("exp_done"), sem("p_masked"), sem("pv_done")
        o_ready = sem("o_ready")
        ot_psum, at_done, atT_psum, atT_ready = sem("ot_psum"), sem("at_done"), sem("atT_psum"), sem("atT_ready")
        mo_psum, xa_added = sem("mo_psum"), sem("xa_added")

        blk = ctx.enter_context(nc.Block())

        def ge(eng, s, v):
            if v > 0:
                eng.wait_ge(s, v)

        def tiles(c):
            return bass.ds(c * TC, TC)

        @blk.sync
        def _(sp):
            x_v = x_in.rearrange("(n p) d -> p n d", p=P)
            sp.dma_start(x[:, 0:TC, :], x_v[:, 0:TC, :]).then_inc(x_first_loaded, 16)
            sp.dma_start(wr[:], w_route).then_inc(ffn_w_loaded, 16)
            sp.dma_start(wg[:], w_gate.rearrange("d (f p) -> d f p", p=P)).then_inc(ffn_w_loaded, 16)
            sp.dma_start(wu[:], w_up.rearrange("d (f p) -> d f p", p=P)).then_inc(ffn_w_loaded, 16)
            sp.dma_start(wd[:], w_down.rearrange("(f p) d -> p f d", p=P)).then_inc(ffn_w_loaded, 16)
            sp.dma_start(x[:, TC:, :], x_v[:, TC:, :]).then_inc(x_rest_loaded, 16)
            for w, src in ((wq, Wq), (wk, Wk), (wv, Wv), (wm, Wm)):
                sp.dma_start(w[:], src).then_inc(attn_w_loaded, 16)
            sp.dma_start(bqk[:, 0:1], bq.rearrange("(p a) -> p a", a=1)).then_inc(attn_w_loaded, 16)
            sp.dma_start(bqk[:, 1:2], bk.rearrange("(p a) -> p a", a=1)).then_inc(attn_w_loaded, 16)
            sp.dma_start(bvb[:], bv.rearrange("(a p) -> a p", a=1).broadcast_to([P, P])).then_inc(attn_w_loaded, 16)
            sp.dma_start(bmr[:], bm.rearrange("(a p) -> a p", a=1)).then_inc(attn_w_loaded, 16)
            sp.wait_ge(pads_done, 1)

            def batch(b):
                for cc in range(CB):
                    sp.wait_ge(part2_ready, b * CB + cc + 1)
                    for s in range(2):
                        sp.dma_start(parts[s, :, :, bass.ds(b * S + cc * CH, CH)].rearrange("a p t -> p a t"),
                                     qp[:, s, :, :]).then_inc(parts_stored, 16)
                sp.wait_ge(parts_stored, (b + 1) * CB * 32)
                for n in range(NQ):
                    rows = slice(n * HQ * HS, (n + 1) * HQ * HS)
                    for a in range(3):
                        for a2 in range(3):
                            r0 = (a * 3 + a2) * HS
                            for s, part, dst in ((0, a, Qs), (1, a2, Ks)):
                                sp.dma_start(dst[r0:r0 + HS, n, :, :],
                                             parts[s, part, rows, bass.ds(b * S, S)]
                                             .rearrange("(h d) t -> d h t", d=HS)).then_inc(stack_loaded[n], 16)
                    sp.dma_start(Qs[SHIFT:SHIFT + 2, n, :, :], zrow[:].unsqueeze(1).broadcast_to([2, HQ, S])).then_inc(stack_loaded[n], 16)
                for n in range(NQ):
                    for half in range(2):
                        turn = TURNS.index(f"max{half}")
                        sp.wait_ge(a_done, (b * NQ + n) * NTURN + turn + 1)
                        for part in range(2):
                            for h in range(HQ):
                                sp.dma_start(Qs[SHIFT + part:SHIFT + part + 1, n, h, half * CH:(half + 1) * CH],
                                             srow[h * TC:(h + 1) * TC, half, part, :]).then_inc(shift_loaded[half], 16)
            for b in range(B):
                batch(b)
            for c in range(NCH):
                sp.wait_ge(ffn_sems[1]["y_added"], c + 1)
                sp.dma_start(out_v[:, c * TC:(c + 1) * TC, :], x[:, c * TC:(c + 1) * TC, :]).then_inc(out_stored, 16)
            sp.wait_ge(out_stored, NCH * 16)

        @blk.gpsimd
        def _(pool):
            done = [0]

            def step(ins):
                done[0] += 1
                ins.then_inc(const_step, 1)
                pool.wait_ge(const_step, done[0])

            pool.memset(ones_row[:], 1.0)
            pool.memset(neg_half[:], -0.5)
            pool.memset(ident[:], 0.0)
            pool.memset(mask[:], 0.0)
            step(pool.memset(sel[:], 0.0))
            pool.affine_select(out=ident[:], in_=ident[:], compare_op=ALU.not_equal, fill=1.0, base=0,
                               pattern=[[-1, P]], channel_multiplier=1)
            last = mask[:, CH - P:CH]
            pool.affine_select(out=last, in_=last, compare_op=ALU.is_ge, fill=BIG, base=0,
                               pattern=[[-1, P]], channel_multiplier=1)
            routed = sel[:, 0:E * MH // P, :].rearrange("r f (s m) -> r f s m", m=MH)
            shared = sel[:, E * MH // P:NF, :]
            for part in range(3):
                pool.affine_select(out=routed, in_=routed, compare_op=ALU.not_equal, fill=1.0, base=-NR * part,
                                   pattern=[[-P // MH, E * MH // P], [-1, P // MH], [0, MH]], channel_multiplier=1)
                step(pool.affine_select(out=shared, in_=shared, compare_op=ALU.not_equal, fill=1.0,
                                        base=-NR * part - E, pattern=[[0, SH // P], [0, P]], channel_multiplier=1))
            step(pool.iota(iota_e[:], pattern=[[1, E]], base=0, channel_multiplier=0, allow_small_or_imprecise_dtypes=True))
            pool.tensor_copy(identb[:], ident[:]).then_inc(const_done, 1)

            def inv_sqrt(ready, done, n):
                pool.wait_ge(ready, n)
                pool.tensor_tensor(rstd[:], ve[:], neg_half[:], ALU.pow).then_inc(done, 1)

            for c in range(NCH):
                inv_sqrt(ffn_sems[0]["ve_ready"], ffn_sems[0]["pow_done"], c + 1)
            pool.wait_ge(ffn_sems[0]["pow_done"], NCH)
            step(pool.memset(Qs[64:P, :, :, :], 0.0))
            step(pool.memset(Ks[64:P, :, :, :], 1.0))
            pool.memset(zrow[:], 0.0)
            step(pool.memset(Vs[:], 0.0))
            pool.memset(Vs[:, :, :, HS:HS + 1], 1.0).then_inc(pads_done, 1)

            def batch(b):
                for cc in range(CB):
                    inv_sqrt(aq_ve, aq_pow, b * CB + cc + 1)
                diag = 0
                for n in range(NQ):
                    for u, (cc, j) in enumerate(UNITS):
                        if unit_shape(cc, j)[2]:
                            U = n * NU + u
                            diag += 1
                            pool.wait_ge(exp_done, (b * NQ * NU + U + 1) * 2)
                            v = pr[:, U % NPB, :, 0:P]
                            pool.affine_select(out=v, in_=v, compare_op=ALU.is_ge, fill=0.0, base=0,
                                               pattern=[[0, HQ], [1, P]], channel_multiplier=-1).then_inc(p_masked, 1)
            for b in range(B):
                batch(b)
            for c in range(NCH):
                inv_sqrt(ffn_sems[1]["ve_ready"], ffn_sems[1]["pow_done"], c + 1)

        @blk.scalar
        def _(act):
            def ffn(s):
                def body(c, first, last):
                    for f in range(NF):
                        g = c * NF + f
                        act.wait_ge(s["g_psum"], g + 1)
                        ge(act, s["su_done"], g - 1)
                        act.activation(sg[:, f % 2, :], ps[:, f % 2, :], ACT.Silu).then_inc(s["sg_ready"], 1)
                        if f == 2 and not first:
                            evac_y(c - 1)
                        if f == 3 and not last:
                            evac_xT(c + 1)
                        if f == 4 and not last:
                            evac_lgT(c + 1)
                        if f == 7 and not last:
                            tanh(c + 1)
                    if not last:
                        evac_cT(c + 1)

                def evac_xT(c):
                    act.wait_ge(s["xT_psum"], c + 1)
                    act.activation(xT[:, c, :], ps[:, 7, :], ACT.Copy).then_inc(s["xT_ready"], 1)

                def evac_lgT(c):
                    act.wait_ge(s["lgT_psum"], c + 1)
                    act.activation(lgT[:], ps[0:NR, 7, :], ACT.Copy).then_inc(s["lgT_ready"], 1)

                def tanh(c):
                    act.wait_ge(s["dz_ready"], c + 1)
                    act.activation(th[:], dz[:], ACT.Tanh, scale=0.5).then_inc(s["th_ready"], 1)

                def evac_cT(c):
                    act.wait_ge(s["cT_psum"], c + 1)
                    act.activation(cT[:, c, :],
                                   ps[0:3 * NR, 7, 0:CH // 2].bitcast(BF16), ACT.Copy).then_inc(s["cT_ready"], 1)

                def evac_y(c):
                    act.wait_ge(s["h_used"], (c + 1) * NF)
                    ge(act, s["yb_psum"], c)
                    act.activation(yT[:], ps[:, 6, :], ACT.Copy).then_inc(s["yT_ready"], 1)

                evac_xT(0)
                evac_lgT(0)
                tanh(0)
                evac_cT(0)
                body(0, True, False)
                for c in range(1, NCH - 1):
                    body(c, False, False)
                body(NCH - 1, False, True)
                evac_y(NCH - 1)

            def batch(b):
                for cc in range(CB):
                    n = b * CB + cc
                    act.wait_ge(aq_xT_psum, n + 1)
                    act.activation(xTa[:, cc, :], ps[:, 4 * cc, :], ACT.Copy).then_inc(aq_xT, 1)
                    act.wait_ge(qk_psum, n + 1)
                    ge(act, part2_ready, n)
                    ge(act, parts_stored, n * 32)
                    for s, (bias, scale) in enumerate(((bqs[:, 0:1], SCALE), (bqk[:, 1:2], 1.0))):
                        act.activation(qf[:, s, :], ps[:, 4 * cc + 1 + s, :], ACT.Identity, bias=bias, scale=scale)
                        ins = act.activation(qp[:, s, 0, :], ps[:, 4 * cc + 1 + s, :], ACT.Identity, bias=bias, scale=scale)
                    ins.then_inc(part0_ready, 1)
                    act.wait_ge(rest_ready, n + 1)
                    act.activation(qp[:, :, 1, :], qr[:], ACT.Copy).then_inc(part1_ready, 1)
                for U in range(NQ * NU):
                    n, (cc, j) = U // NU, UNITS[U % NU]
                    w = unit_shape(cc, j)[1]
                    for hp in range(2):
                        k = (b * NQ * NU + U) * 2 + hp
                        act.wait_ge(st_psum, k + 1)
                        if hp == 0:
                            ge(act, pv_done, b * NQ * NU + U - NPB + 1 if U >= NPB else b * NQ * NU)
                        act.activation(pr[:, U % NPB, 2 * hp:2 * hp + 2, 0:w], ps[:, 2 * hp:2 * hp + 2, 0:w],
                                       ACT.Exp).then_inc(exp_done, 1)
                    if U % NU == 4 or (U % NU == 0 and U > 0):
                        evac_o(b, n * 2 - (1 if U % NU == 0 else 0))
                evac_o(b, 2 * NQ - 1)
                for i in range(TB):
                    m = b * TB + i
                    act.wait_ge(atT_psum, m + 1)
                    ge(act, mo_psum, m - 1 if i else b * TB)
                    act.activation(atT[:, i % 2, :], ps[:, 2 + i % 2, 0:P], ACT.Copy).then_inc(atT_ready, 1)

            def evac_o(b, k):
                n, cc = k // 2, k % 2
                act.wait_ge(pv_done, (b * NQ + n) * NU + (TC if cc == 0 else NU))
                act.activation(oT[:, n, cc * CH:(cc + 1) * CH], ps[:, 6 + cc, :], ACT.Copy).then_inc(o_ready, 1)

            act.wait_ge(attn_w_loaded, 8 * 16)
            act.mul(bqs[:], bqk[:, 0:1], SCALE).then_inc(bqs_ready, 1)
            ffn(ffn_sems[0])
            act.wait_ge(bqs_ready, 1)
            for b in range(B):
                batch(b)
            ffn(ffn_sems[1])

        @blk.tensor
        def _(pe):
            def ffn(s):
                def turn_x(c):
                    pe.wait_ge(s["xn_ready"], c + 1)
                    for t in range(TC):
                        mm_ = pe.transpose(ps[:, 7, t * P:(t + 1) * P], xn[:, t, :], ident[:])
                    mm_.then_inc(s["xT_psum"], 1)

                def logits(c):
                    pe.wait_ge(s["xT_ready"], c + 1)
                    pe.matmul(ps[0:NR, 7, :], wr[:], xT[:, c, :], start=True, stop=True).then_inc(s["lgT_psum"], 1)

                def turn_logits(c):
                    pe.wait_ge(s["lgT_ready"], c + 1)
                    for t in range(TC):
                        mm_ = pe.transpose(ps[:, 7, t * NR:(t + 1) * NR], lgT[:, t * P:(t + 1) * P], ident[0:NR, 0:NR])
                    mm_.then_inc(s["lg_psum"], 1)

                def turn_weights(c):
                    pe.wait_ge(s["cp_ready"], c + 1)
                    for t in range(TC):
                        mm_ = pe.transpose(ps[0:3 * NR, 7, 0:CH // 2].bitcast(BF16)[:, t * P:(t + 1) * P],
                                           cp[:, t, :, :].rearrange("p a r -> p (a r)"), identb[:])
                    mm_.then_inc(s["cT_psum"], 1)

                def up(c, f):
                    g = c * NF + f
                    ge(pe, s["sg_ready"], g - 1)
                    pe.matmul(ps[:, f % 2, :], wg[:, f, :], xT[:, c, :], start=True, stop=True).then_inc(s["g_psum"], 1)
                    ge(pe, s["su_done"], g - 1)
                    pe.matmul(ps[:, 2 + f % 2, :], wu[:, f, :], xT[:, c, :], start=True, stop=True)
                    ge(pe, s["h_ready"], g - 1)
                    pe.matmul(ps[:, 4 + f % 2, :], sel[:, f, :], cT[:, c, :], start=True, stop=True)\
                        .then_inc(s["uc_psum"], 1)

                def down(c, f):
                    pe.wait_ge(s["h_ready"], c * NF + f + 1)
                    if f == 0:
                        ge(pe, s["yT_ready"], c)
                    pe.matmul(ps[:, 6, :], wd[:, f, :], hh[:, f % 2, :], start=f == 0, stop=f == NF - 1)\
                        .then_inc(s["h_used"], 1)

                def turn_y(c):
                    pe.wait_ge(s["yT_ready"], c + 1)
                    for t in range(TC):
                        mm_ = pe.transpose(ps[:, 7, t * P:(t + 1) * P], yT[:, t * P:(t + 1) * P], ident[:])
                    mm_.then_inc(s["yb_psum"], 1)

                def body(c, first, last):
                    pe.wait_ge(s["cT_ready"], c + 1)
                    for f in range(NF):
                        up(c, f)
                        if f < 2:
                            if not first:
                                down(c - 1, NF - 2 + f)
                        else:
                            down(c, f - 2)
                        if f == 2 and not last:
                            turn_x(c + 1)
                        if f == 3 and not last:
                            logits(c + 1)
                        if f == 4 and not last:
                            turn_logits(c + 1)
                        if f == 5 and not first:
                            if not last:
                                pe.wait_ge(s["lg_read"], c + 2)
                            turn_y(c - 1)
                        if f == 9 and not last:
                            if not first:
                                pe.wait_ge(s["y_added"], c)
                            turn_weights(c + 1)

                turn_x(0)
                logits(0)
                turn_logits(0)
                turn_weights(0)
                body(0, True, False)
                for c in range(1, NCH - 1):
                    body(c, False, False)
                body(NCH - 1, False, True)
                down(NCH - 1, NF - 2)
                down(NCH - 1, NF - 1)
                pe.wait_ge(s["y_added"], NCH - 1)
                turn_y(NCH - 1)
                pe.wait_ge(s["y_added"], NCH)

            def project(b):
                for cc in range(CB):
                    n = b * CB + cc
                    pe.wait_ge(aq_xn, n + 1)
                    for t in range(TC):
                        mm_ = pe.transpose(ps[:, 4 * cc, t * P:(t + 1) * P], xn[:, t, :], ident[:])
                    mm_.then_inc(aq_xT_psum, 1)
                    pe.wait_ge(aq_xT, n + 1)
                    pe.matmul(ps[:, 4 * cc + 1, :], wq[:], xTa[:, cc, :], start=True, stop=True)
                    pe.matmul(ps[:, 4 * cc + 2, :], wk[:], xTa[:, cc, :], start=True, stop=True).then_inc(qk_psum, 1)
                    for t in range(TC):
                        mm_ = pe.matmul(ps[:, 4 * cc + 3, t * P:(t + 1) * P], xTa[:, cc, t * P:(t + 1) * P], wv[:],
                                        start=True, stop=True)
                    mm_.then_inc(v_psum, 1)

            def a_turn(b, n, k):
                a = (b * NQ + n) * NTURN + k
                ge(pe, a_done, a - 1 if n or k > 1 else b * NQ * NTURN)
                bank = 4 + k % 2
                turn = TURNS[k]
                if turn == "max0" or turn == "max1":
                    if turn == "max0":
                        pe.wait_ge(a_done, (b * NQ + n) * NTURN + LAST_MAX0)
                    else:
                        pe.wait_ge(max1_ready, b * NQ + n + 1)
                    pe.transpose(ps[0:HQ * TC, bank, 0:P],
                                 mmx[:, n % 2, int(turn[3]), :, :].rearrange("p h i -> p (h i)"), ident[:]).then_inc(a_psum, 1)
                    return
                half, h, i, piece = turn
                q = half * CH + i * P
                w = CH if half > piece else (i + 1) * P
                pe.matmul(ps[:, bank, 0:w], Qs[:, n, h, q:q + P], Ks[:, n, h, piece * CH:piece * CH + w],
                          start=True, stop=True).then_inc(a_psum, 1)

            def st_pair(b, U, hp):
                n, (cc, j) = U // NU, UNITS[U % NU]
                k = (b * NQ * NU + U) * 2 + hp
                ge(pe, exp_done, k - 1 if U else b * NQ * NU * 2)
                if hp == 0 and (j == 0):
                    pe.wait_ge(shift_loaded[cc], (b * NQ + n + 1) * 2 * HQ * 16)
                q0, w, _ = unit_shape(cc, j)
                for x_ in range(2):
                    h = 2 * hp + x_
                    mm_ = pe.matmul(ps[:, h, 0:w], Ks[:, n, h, j * P:(j + 1) * P], Qs[:, n, h, q0:q0 + w],
                                    start=True, stop=True)
                mm_.then_inc(st_psum, 1)

            def pv(b, U):
                n, (cc, j) = U // NU, UNITS[U % NU]
                q0, w, diag = unit_shape(cc, j)
                pe.wait_ge(exp_done, (b * NQ * NU + U + 1) * 2)
                if diag:
                    pe.wait_ge(p_masked, (b * NQ + n) * TB + j + 1)
                if j == 0:
                    ge(pe, o_ready, b * 2 * NQ + max(0, 2 * n + cc - 1))
                for h in range(HQ):
                    mm_ = pe.matmul(ps[VC * h:VC * (h + 1), 6 + cc, CH - w:CH], Vs[:, j, n * HQ + h, :],
                                    pr[:, U % NPB, h, 0:w], start=j == 0, stop=j == TC * (cc + 1) - 1,
                                    tile_position=(0, VC * h))
                mm_.then_inc(pv_done, 1)

            def batch(b):
                project(b)
                pe.wait_ge(part2_ready, (b + 1) * CB)
                pe.wait_ge(v_ready, (b + 1) * CB)
                pe.wait_ge(stack_loaded[0], (b + 1) * 19 * 16)
                for k in range(NTURN - 1):
                    a_turn(b, 0, k)
                for U in range(NQ * NU):
                    n, u = U // NU, U % NU
                    more = n + 1 < NQ
                    if u == 0 and more:
                        pe.wait_ge(stack_loaded[n + 1], (b + 1) * 19 * 16)
                    st_pair(b, U, 0)
                    if u == 0:
                        a_turn(b, n, NTURN - 1)
                    if more:
                        for k in range(4 * u, 4 * u + 2):
                            a_turn(b, n + 1, k)
                    st_pair(b, U, 1)
                    if more:
                        for k in range(4 * u + 2, 4 * u + 4):
                            a_turn(b, n + 1, k)
                        if u == NU - 1:
                            a_turn(b, n + 1, NTURN - 2)
                    if U:
                        pv(b, U - 1)
                pv(b, NQ * NU - 1)
                pe.wait_ge(o_ready, (b + 1) * 2 * NQ)
                for i in range(TB + 2):
                    if i < TB:
                        ge(pe, at_done, b * TB + max(0, i - 1))
                        for n in range(NQ):
                            mm_ = pe.transpose(ps[:, i % 2, n * P:(n + 1) * P], oT[:, n, i * P:(i + 1) * P], ident[:])
                        mm_.then_inc(ot_psum, 1)
                    if 0 <= i - 1 < TB:
                        k = i - 1
                        pe.wait_ge(at_done, b * TB + k + 1)
                        ge(pe, atT_ready, b * TB + max(0, k - 1))
                        pe.transpose(ps[:, 2 + k % 2, 0:P], at[:, k % 2, :], ident[:]).then_inc(atT_psum, 1)
                    if i >= 2:
                        k = i - 2
                        pe.wait_ge(atT_ready, b * TB + k + 1)
                        ge(pe, xa_added, b * TB + max(0, k - 1))
                        pe.matmul(ps[:, 4 + k % 2, 0:P], atT[:, k % 2, :], wm[:], start=True, stop=False)
                        pe.matmul(ps[:, 4 + k % 2, 0:P], ones_row[:], bmr[:], start=False, stop=True).then_inc(mo_psum, 1)
                pe.wait_ge(xa_added, (b + 1) * TB)

            pe.wait_ge(const_done, 1)
            pe.wait_ge(ffn_w_loaded, 4 * 16)
            ffn(ffn_sems[0])
            pe.wait_ge(attn_w_loaded, 8 * 16)
            pe.wait_ge(pads_done, 1)
            for b in range(B):
                batch(b)
            ffn(ffn_sems[1])

        @blk.vector
        def _(dve):
            steps = [0]

            def step(ins):
                steps[0] += 1
                ins.then_inc(vstep, 1)
                dve.wait_ge(vstep, steps[0])

            def layernorm(c, n, ready, done, xn_ready):
                for t in range(TC):
                    ins = dve.bn_stats(st[:, t, :], x[:, bass.ds(c * TC + t, 1), :].rearrange("p a d -> p (a d)"))
                step(ins)
                for t in range(TC):
                    ins = dve.bn_aggr(mv[:, t, :], st[:, t, :])
                step(ins)
                dve.tensor_scalar(ve[:], mv[:, :, 1], EPS, None, ALU.add).then_inc(ready, 1)
                dve.wait_ge(done, n + 1)
                for t in range(TC):
                    ins = dve.tensor_scalar(xn[:, t, :], x[:, bass.ds(c * TC + t, 1), :].rearrange("p a d -> p (a d)"),
                                            mv[:, t, 0:1], rstd[:, t:t + 1], ALU.subtract, ALU.mult)
                ins.then_inc(xn_ready, 1)

            def ffn(s, load):
                def norm(c):
                    if load:
                        dve.wait_ge(x_first_loaded if c == 0 else x_rest_loaded, 16)
                    ge(dve, s["xT_psum"], c)
                    layernorm(c, c, s["ve_ready"], s["pow_done"], s["xn_ready"])

                def route(c):
                    dve.wait_ge(s["lg_psum"], c + 1)
                    dve.tensor_copy(lg[:], ps[:, 7, 0:TC * NR].rearrange("p (t r) -> p t r", r=NR)).then_inc(s["lg_read"], 1)
                    dve.wait_ge(s["lg_read"], c + 1)
                    for t in range(TC):
                        ins = dve.max(mx8[:, t, :], lg[:, t, 0:E])
                    step(ins)
                    for t in range(TC):
                        ins = dve.max_index(ix8[:, t, :], mx8[:, t, :], lg[:, t, 0:E])
                    step(ins)
                    dve.tensor_tensor(dz[:, 0, :], mx8[:, :, 1], mx8[:, :, 0], ALU.subtract)
                    dve.tensor_copy(dz[:, 1, :], lg[:, :, E]).then_inc(s["dz_ready"], 1)
                    step(dve.tensor_copy(ixf[:], ix8[:, :, 0:2]))
                    experts = iota_e[:].unsqueeze(1).broadcast_to([P, TC, E])
                    dve.tensor_tensor(e1[:], experts, ixf[:, :, 0:1].broadcast_to([P, TC, E]), ALU.is_equal)
                    step(dve.tensor_tensor(e2[:], experts, ixf[:, :, 1:2].broadcast_to([P, TC, E]), ALU.is_equal))

                def weigh(c):
                    dve.wait_ge(s["th_ready"], c + 1)
                    step(dve.tensor_scalar(rw[:, 0:2, :], th[:], 1.0, 0.25, ALU.add, ALU.mult))
                    dve.tensor_copy(cf[:, :, E], rw[:, 1, :])
                    step(dve.tensor_scalar(rw[:, 2, :], rw[:, 0, :], -1.0, 0.5, ALU.mult, ALU.add))
                    dve.tensor_tensor(e1[:], e1[:], rw[:, 2, :].unsqueeze(2).broadcast_to([P, TC, E]), ALU.mult)
                    step(dve.tensor_tensor(e2[:], e2[:], rw[:, 0, :].unsqueeze(2).broadcast_to([P, TC, E]), ALU.mult))
                    step(dve.tensor_tensor(cf[:, :, 0:E], e1[:], e2[:], ALU.add))
                    ge(dve, s["cT_psum"], c)
                    step(dve.tensor_copy(cp[:, :, 0, :], cf[:]))
                    step(dve.tensor_tensor(cr[:], cf[:], cp[:, :, 0, :], ALU.subtract))
                    step(dve.tensor_copy(cp[:, :, 1, :], cr[:]))
                    dve.tensor_tensor(cp[:, :, 2, :], cr[:], cp[:, :, 1, :], ALU.subtract).then_inc(s["cp_ready"], 1)

                def times_u(c, f):
                    g = c * NF + f
                    dve.wait_ge(s["sg_ready"], g + 1)
                    dve.wait_ge(s["uc_psum"], g + 1)
                    dve.tensor_tensor(su[:, f % 2, :], ps[:, 2 + f % 2, :], sg[:, f % 2, :], ALU.mult).then_inc(s["su_done"], 1)

                def times_c(c, f):
                    g = c * NF + f
                    dve.wait_ge(s["su_done"], g + 1)
                    ge(dve, s["h_used"], g - 1)
                    dve.tensor_tensor(hh[:, f % 2, :], ps[:, 4 + f % 2, :], su[:, f % 2, :], ALU.mult).then_inc(s["h_ready"], 1)

                def add_y(c):
                    dve.wait_ge(s["yb_psum"], c + 1)
                    xs = x[:, bass.ds(c * TC, TC), :]
                    dve.tensor_tensor(xs, ps[:, 7, :].rearrange("p (t d) -> p t d", d=D), xs, ALU.add).then_inc(s["y_added"], 1)

                def body(c, first, last):
                    for f in range(NF):
                        times_u(c, f)
                        if f:
                            times_c(c, f - 1)
                        elif not first:
                            times_c(c - 1, NF - 1)
                        if f == 1 and not last:
                            norm(c + 1)
                        if f == 5 and not last:
                            route(c + 1)
                        if f == 6 and not first:
                            add_y(c - 1)
                        if f == 8 and not last:
                            weigh(c + 1)

                norm(0)
                route(0)
                weigh(0)
                body(0, True, False)
                for c in range(1, NCH - 1):
                    body(c, False, False)
                body(NCH - 1, False, True)
                times_c(NCH - 1, NF - 1)
                add_y(NCH - 1)

            def a_turn(b, n, k):
                dve.wait_ge(a_psum, (b * NQ + n) * NTURN + k + 1)
                bank, turn = 4 + k % 2, TURNS[k]
                if turn == "max0" or turn == "max1":
                    half = int(turn[3])
                    ge(dve, shift_loaded[half], (b * NQ + n) * 2 * HQ * 16)
                    step(dve.tensor_scalar(srow[:, half, 0, :], ps[0:HQ * TC, bank, 0:P], -1.0, None, ALU.mult))
                    dve.scalar_tensor_tensor(out=srow[:, half, 1, :], in0=ps[0:HQ * TC, bank, 0:P], scalar=-1.0,
                                             in1=srow[:, half, 0, :], op0=ALU.mult, op1=ALU.subtract).then_inc(a_done, 1)
                    return
                half, h, i, piece = turn
                dst = m2[:, n % 2, h, i, piece:piece + 1] if half else mmx[:, n % 2, 0, h, i:i + 1]
                if half > piece:
                    dve.reduce_max(dst, ps[:, bank, :], AX.X).then_inc(a_done, 1)
                else:
                    w = (i + 1) * P
                    dve.tensor_tensor_reduce(out=junk[:, k % 2, 0:w], in0=ps[:, bank, 0:w], in1=mask[:, CH - w:CH], scale=1.0,
                                             scalar=-3e38, op0=ALU.add, op1=ALU.max, accum_out=dst).then_inc(a_done, 1)
                if k == NTURN - 2:
                    dve.wait_ge(a_done, (b * NQ + n) * NTURN + NTURN - 1)
                    dve.tensor_tensor(mmx[:, n % 2, 1, :, :], m2[:, n % 2, :, :, 0], m2[:, n % 2, :, :, 1],
                                      ALU.max).then_inc(max1_ready, 1)

            def batch(b):
                for cc in range(CB):
                    n = b * CB + cc
                    ge(dve, aq_xT_psum, n)
                    layernorm(b * CB + cc, n, aq_ve, aq_pow, aq_xn)
                    if cc:
                        split(b, 0)
                split(b, 1)
                for k in range(NTURN - 1):
                    a_turn(b, 0, k)
                for n in range(NQ):
                    a_turn(b, n, NTURN - 1)
                    if n + 1 < NQ:
                        for k in range(NTURN - 1):
                            a_turn(b, n + 1, k)
                for i in range(TB + 1):
                    if i < TB:
                        m = b * TB + i
                        dve.wait_ge(ot_psum, m + 1)
                        heads = ps[:, i % 2, :].rearrange("p (h v) -> p h v", v=VC)
                        step(dve.reciprocal(rec[:, i % 2, :], heads[:, :, HS]))
                        ge(dve, atT_psum, b * TB + max(0, i - 1))
                        dve.tensor_tensor(at[:, i % 2, :].rearrange("p (h d) -> p h d", d=HS), heads[:, :, 0:HS],
                                          rec[:, i % 2, :].unsqueeze(2).broadcast_to([P, H, HS]), ALU.mult).then_inc(at_done, 1)
                    if i:
                        k = i - 1
                        dve.wait_ge(mo_psum, b * TB + k + 1)
                        xs = x[:, bass.ds(b * TB + k, 1), :].rearrange("p a d -> p (a d)")
                        dve.tensor_tensor(xs, ps[:, 4 + k % 2, 0:P], xs, ALU.add).then_inc(xa_added, 1)

            def split(b, cc):
                n = b * CB + cc
                dve.wait_ge(part0_ready, n + 1)
                dve.tensor_tensor(qr[:], qf[:], qp[:, :, 0, :], ALU.subtract).then_inc(rest_ready, 1)
                dve.wait_ge(v_psum, n + 1)
                dve.tensor_tensor(Vs[:, cc * TC:(cc + 1) * TC, :, 0:HS],
                                  ps[:, 4 * cc + 3, :].rearrange("p (t h d) -> p t h d", h=H, d=HS),
                                  bvb[:].rearrange("p (h d) -> p h d", d=HS).unsqueeze(1).broadcast_to([P, TC, H, HS]),
                                  ALU.add).then_inc(v_ready, 1)
                dve.wait_ge(part1_ready, n + 1)
                dve.tensor_tensor(qp[:, :, 2, :], qr[:], qp[:, :, 1, :], ALU.subtract).then_inc(part2_ready, 1)

            dve.wait_ge(const_done, 1)
            ffn(ffn_sems[0], True)
            dve.wait_ge(ffn_sems[0]["y_added"], NCH)
            dve.wait_ge(attn_w_loaded, 8 * 16)
            dve.wait_ge(pads_done, 1)
            for b in range(B):
                batch(b)
            dve.wait_ge(xa_added, NT)
            ffn(ffn_sems[1], False)


_OUT = ("out_dram", (B, S, D))


def kernel(**inputs):
    import numpy as np
    import concourse.bacc as bacc
    from concourse.bass_utils import run_bass_kernel_spmd

    a = {k.removeprefix("L0_"): np.asarray(v) for k, v in inputs.items()}
    hid = lambda e, s: np.concatenate([e.reshape(E * MH, D), s], 0).T
    arrays = {
        "x": a["attn_x"].reshape(T, D),
        "w_gate": hid(a["ffn_We_gate"], a["ffn_Ws_gate"]),
        "w_up": hid(a["ffn_We_up"], a["ffn_Ws_up"]),
        "w_down": np.concatenate([a["ffn_We_down"].transpose(0, 2, 1).reshape(E * MH, D), a["ffn_Ws_down"].T], 0),
        "w_route": np.concatenate([a["ffn_Wg"], a["ffn_Wsg"]], 0).T,
    }
    for n in ("Wq", "bq", "Wk", "bk", "Wv", "bv", "Wm", "bm"):
        arrays[n] = a["attn_" + n]
    arrays = {f"in_{n}": np.ascontiguousarray(v) for n, v in arrays.items()}
    nc = bacc.Bacc("TRN2", target_bir_lowering=False, num_devices=1)
    args = [nc.dram_tensor(n, v.shape, mybir.dt.from_np(v.dtype), kind="ExternalInput").ap() for n, v in arrays.items()]
    args.append(nc.dram_tensor(_OUT[0], (T, D), F32, kind="ExternalOutput").ap())
    macaron(nc, *args)
    r = run_bass_kernel_spmd(nc, [arrays], core_ids=[0])
    return r.results[0][_OUT[0]].reshape(_OUT[1])
```

```python
import concourse.bass as bass
from concourse import mybir
from contextlib import ExitStack

F32 = mybir.dt.float32
BF16 = mybir.dt.bfloat16
U32 = mybir.dt.uint32
ALU = mybir.AluOpType
ACT = mybir.ActivationFunctionType
AX = mybir.AxisListType

P = 128
D = 128
B, S = 2, 1024
T = B * S
NT = T // P
CH = 512
TC = CH // P
NCH = T // CH
E, MH, SH = 16, 64, 256
EH = E * MH + SH
NF = EH // P
NR = E + 1
H, HS = 16, 8
SCALE = HS ** -0.5
NQ = 4
HQ = H // NQ
TB = S // P
CB = S // CH
ROWS = 9 * HS
SHIFT = ROWS
VC = 16
EPS = 1e-5
BIG = -1e30

HALF0 = [(0, h, i, 0) for i in range(TC) for h in range(HQ)]
HALF1 = [(1, h, i, p) for i in range(TC) for h in range(HQ) for p in range(2)]
TURNS = HALF0 + HALF1[:2] + ["max0"] + HALF1[2:] + ["max1"]
NTURN = len(TURNS)
LAST_MAX0 = 16
UNITS = [(cc, j) for cc in range(CB) for j in range(TC * (cc + 1))]
NU = len(UNITS)
NN = B * NQ
NPB = 3

G_BANK, U_BANKS, C_BANKS, Y_BANK, FRONT_BANK, SIDE_BANK = 0, (1, 2), (3, 4), 5, 6, 7
O_BANK, A_BANKS, ST_BANKS = 0, (1, 2, 3, 4), (5, 6, 7)
FRONT_BANK2 = 3


def unit_shape(cc, j):
    q0 = max(CH * cc, P * j)
    return q0, CH * (cc + 1) - q0, P * j >= CH * cc


def macaron(nc, x_in, w_gate, w_up, w_down, w_route, Wq, bq, Wk, bk, Wv, bv, Wm, bm, out):
    ctx = ExitStack()
    with ctx:
        def sb(name, shape, dt=F32):
            return ctx.enter_context(nc.sbuf_tensor(name, shape, dt))

        def sem(name):
            return ctx.enter_context(nc.semaphore(name))

        x = sb("x", [P, NT, D])
        wg = sb("wg", [P, NF, P])
        wu = sb("wu", [P, NF, P])
        wd = sb("wd", [P, NF, D])
        wr = sb("wr", [P, NR])
        wq = sb("wq", [P, P])
        wk = sb("wk", [P, P])
        wv = sb("wv", [P, P])
        wm = sb("wm", [P, P])
        bqk = sb("bqk", [P, 2])
        bqs = sb("bqs", [P, 1])
        bvb = sb("bvb", [P, P])
        bmr = sb("bmr", [1, P])
        ones_row = sb("ones_row", [1, P])
        ident = sb("ident", [P, P])
        identb = sb("identb", [P, P], BF16)
        sel = sb("sel", [3 * NR, NF, P], BF16)
        iota_e = sb("iota_e", [P, E])
        neg_half = sb("neg_half", [P, TC])
        mask = sb("mask", [P, CH])
        st = sb("st", [P, 2, TC, 6])
        mv = sb("mv", [P, 2, TC, 2])
        ve = sb("ve", [P, 2, TC])
        rstd = sb("rstd", [P, 2, TC])
        xn = sb("xn", [P, 2, TC, D])
        xT = sb("xT", [P, 2, CH])
        xTa = sb("xTa", [P, CH])
        lgT = sb("lgT", [NR, CH])
        lg = sb("lg", [P, TC, NR])
        mx8 = sb("mx8", [P, TC, 8])
        ix8 = sb("ix8", [P, TC, 8], U32)
        ixf = sb("ixf", [P, TC, 2])
        dz = sb("dz", [P, 2, TC])
        th = sb("th", [P, 2, TC])
        rw = sb("rw", [P, 3, TC])
        e1 = sb("e1", [P, TC, E])
        e2 = sb("e2", [P, TC, E])
        cf = sb("cf", [P, TC, NR])
        cr = sb("cr", [P, TC, NR])
        cp = sb("cp", [P, TC, 3, NR], BF16)
        cT = sb("cT", [3 * NR, 2, CH], BF16)
        Qs = sb("Qs", [P, NQ, HQ, S], BF16)
        Ks = sb("Ks", [P, NQ, HQ, S], BF16)
        zrow = sb("zrow", [2, S], BF16)
        Vs = sb("Vs", [P, B, TB, H, VC])
        junk = sb("junk", [P, len(A_BANKS), CH], BF16)
        mmx = sb("mmx", [P, 2, 2, HQ, TC])
        m2 = sb("m2", [P, 2, HQ, TC, 2])
        srow = sb("srow", [HQ * TC, 2, 2, P], BF16)
        oT = sb("oT", [P, B, NQ, S])
        rec = sb("rec", [P, TC, H])
        at = sb("at", [P, TC, P])
        atT = sb("atT", [P, CH])
        pr = sb("pr", [P, NPB, HQ, CH])
        hid = pr[:].rearrange("p b h t -> p (b h) t")
        sg, su, hh, yT = hid[:, 0:2, :], hid[:, 2:5, :], hid[:, 5:7, :], hid[:, 7, :]
        spare = oT[:, 1, :, :].rearrange("p n t -> p (n t)")
        qf = spare[:, 0:2 * CH].rearrange("p (s t) -> p s t", s=2)
        qr = spare[:, 2 * CH:4 * CH].rearrange("p (s t) -> p s t", s=2)
        qp = spare[:, 4 * CH:7 * CH].bitcast(BF16).rearrange("p (s a t) -> p s a t", s=2, a=3)

        ps = ctx.enter_context(nc.psum_tensor("ps", [P, 8, CH], F32))
        parts = nc.dram_tensor("parts", [2, 3, P, T], BF16, kind="Internal").ap()
        out_v = out.rearrange("(n p) d -> p n d", p=P)

        x_first_loaded = sem("x_first_loaded")
        x_rest_loaded = sem("x_rest_loaded")
        wr_loaded = sem("wr_loaded")
        ffn_w_loaded = sem("ffn_w_loaded")
        attn_w_loaded = sem("attn_w_loaded")
        const_step = sem("const_step")
        const_done = sem("const_done")
        pads_done = sem("pads_done")
        vpads_done = sem("vpads_done")
        vstep = sem("vstep")
        out_stored = sem("out_stored")
        FFN_SEMS = ("ve_ready", "pow_done", "xn_ready", "xT_psum", "xT_ready", "lgT_psum", "lgT_ready",
                    "lg_psum", "lg_read", "dz_ready", "th_ready", "cp_ready", "cT_psum", "cT_ready",
                    "g_psum", "u_psum", "c_psum", "sg_ready", "su_done", "h_ready", "h_used",
                    "yT_ready", "yb_psum", "y_added")
        ffn_sems = [{n: sem(f"{n}{k}") for n in FFN_SEMS} for k in range(2)]
        bqs_ready = sem("bqs_ready")
        ve2_ready, pow2_done, xn2_ready = sem("ve2_ready"), sem("pow2_done"), sem("xn2_ready")
        xTa_psum, xTa_ready = sem("xTa_psum"), sem("xTa_ready")
        qk_psum, v_psum = sem("qk_psum"), sem("v_psum")
        part0_ready, rest_ready = sem("part0_ready"), sem("rest_ready")
        part1_ready, part2_ready = sem("part1_ready"), sem("part2_ready")
        v_ready = sem("v_ready")
        parts_stored = sem("parts_stored")
        stack_loaded = [sem(f"stack_loaded{n}") for n in range(NQ)]
        shift_loaded = [sem(f"shift_loaded{h}") for h in range(2)]
        a_psum, a_done, max1_ready = sem("a_psum"), sem("a_done"), sem("max1_ready")
        st_psum, exp_done, p_masked, pv_done = sem("st_psum"), sem("exp_done"), sem("p_masked"), sem("pv_done")
        o_ready = sem("o_ready")
        ot_psum, at_done = sem("ot_psum"), sem("at_done")
        atT_psum, atT_ready = sem("atT_psum"), sem("atT_ready")
        mo_psum, xa_added = sem("mo_psum"), sem("xa_added")

        blk = ctx.enter_context(nc.Block())

        def ge(eng, s, v):
            if v > 0:
                eng.wait_ge(s, v)

        def xs(c):
            return x[:, c * TC:(c + 1) * TC, :]

        @blk.sync
        def _(sp):
            x_v = x_in.rearrange("(n p) d -> p n d", p=P)
            sp.dma_start(x[:, 0:TC, :], x_v[:, 0:TC, :]).then_inc(x_first_loaded, 16)
            sp.dma_start(wr[:], w_route).then_inc(wr_loaded, 16)
            sp.dma_start(wg[:], w_gate.rearrange("d (f p) -> d f p", p=P)).then_inc(ffn_w_loaded, 16)
            sp.dma_start(wu[:], w_up.rearrange("d (f p) -> d f p", p=P)).then_inc(ffn_w_loaded, 16)
            sp.dma_start(wd[:], w_down.rearrange("(f p) d -> p f d", p=P)).then_inc(ffn_w_loaded, 16)
            sp.dma_start(x[:, TC:, :], x_v[:, TC:, :]).then_inc(x_rest_loaded, 16)
            for w, src in ((wq, Wq), (wk, Wk), (wv, Wv), (wm, Wm)):
                sp.dma_start(w[:], src).then_inc(attn_w_loaded, 16)
            sp.dma_start(bqk[:, 0:1], bq.rearrange("(p a) -> p a", a=1)).then_inc(attn_w_loaded, 16)
            sp.dma_start(bqk[:, 1:2], bk.rearrange("(p a) -> p a", a=1)).then_inc(attn_w_loaded, 16)
            sp.dma_start(bvb[:], bv.rearrange("(a p) -> a p", a=1).broadcast_to([P, P])).then_inc(attn_w_loaded, 16)
            sp.dma_start(bmr[:], bm.rearrange("(a p) -> a p", a=1)).then_inc(attn_w_loaded, 16)

            def store_parts(k):
                sp.wait_ge(part2_ready, k + 1)
                for s in range(2):
                    sp.dma_start(parts[s, :, :, k * CH:(k + 1) * CH].rearrange("a p t -> p a t"),
                                 qp[:, s, :, :]).then_inc(parts_stored, 16)

            def load_stack(b, n):
                rows = slice(n * HQ * HS, (n + 1) * HQ * HS)
                for a in range(3):
                    for a2 in range(3):
                        r0 = (a * 3 + a2) * HS
                        for s, part, dst in ((0, a, Qs), (1, a2, Ks)):
                            sp.dma_start(dst[r0:r0 + HS, n, :, :],
                                         parts[s, part, rows, b * S:(b + 1) * S]
                                         .rearrange("(h d) t -> d h t", d=HS)).then_inc(stack_loaded[n], 16)
                sp.dma_start(Qs[SHIFT:SHIFT + 2, n, :, :], zrow[:].unsqueeze(1).broadcast_to([2, HQ, S]))\
                    .then_inc(stack_loaded[n], 16)

            def load_shift(N, half):
                sp.wait_ge(a_done, N * NTURN + TURNS.index(f"max{half}") + 1)
                for part in range(2):
                    for h in range(HQ):
                        sp.dma_start(Qs[SHIFT + part:SHIFT + part + 1, N % NQ, h, half * CH:(half + 1) * CH],
                                     srow[h * TC:(h + 1) * TC, half, part, :]).then_inc(shift_loaded[half], 16)

            for k in range(CB):
                store_parts(k)
            sp.wait_ge(parts_stored, CB * 32)
            sp.wait_ge(pads_done, 1)
            for n in range(NQ):
                load_stack(0, n)
            for k in range(CB, NCH):
                store_parts(k)
            sp.wait_ge(parts_stored, NCH * 32)
            load_shift(0, 0)
            for N in range(NN):
                load_shift(N, 1)
                if 1 <= N <= NQ:
                    sp.wait_ge(pv_done, N * NU)
                    load_stack(1, N - 1)
                if N + 1 < NN:
                    load_shift(N + 1, 0)
            for c in range(NCH):
                sp.wait_ge(ffn_sems[1]["y_added"], c + 1)
                sp.dma_start(out_v[:, c * TC:(c + 1) * TC, :], xs(c)).then_inc(out_stored, 16)
            sp.wait_ge(out_stored, NCH * 16)

        @blk.gpsimd
        def _(pool):
            done = [0]

            def step(ins):
                done[0] += 1
                ins.then_inc(const_step, 1)
                pool.wait_ge(const_step, done[0])

            pool.memset(ones_row[:], 1.0)
            pool.memset(neg_half[:], -0.5)
            pool.memset(ident[:], 0.0)
            pool.memset(mask[:], 0.0)
            step(pool.memset(sel[:], 0.0))
            pool.affine_select(out=ident[:], in_=ident[:], compare_op=ALU.not_equal, fill=1.0, base=0,
                               pattern=[[-1, P]], channel_multiplier=1)
            last = mask[:, CH - P:CH]
            pool.affine_select(out=last, in_=last, compare_op=ALU.is_ge, fill=BIG, base=0,
                               pattern=[[-1, P]], channel_multiplier=1)
            routed = sel[:, 0:E * MH // P, :].rearrange("r f (s m) -> r f s m", m=MH)
            shared = sel[:, E * MH // P:NF, :]
            for part in range(3):
                pool.affine_select(out=routed, in_=routed, compare_op=ALU.not_equal, fill=1.0, base=-NR * part,
                                   pattern=[[-P // MH, E * MH // P], [-1, P // MH], [0, MH]], channel_multiplier=1)
                step(pool.affine_select(out=shared, in_=shared, compare_op=ALU.not_equal, fill=1.0,
                                        base=-NR * part - E, pattern=[[0, SH // P], [0, P]], channel_multiplier=1))
            step(pool.iota(iota_e[:], pattern=[[1, E]], base=0, channel_multiplier=0, allow_small_or_imprecise_dtypes=True))
            pool.tensor_copy(identb[:], ident[:]).then_inc(const_done, 1)

            def inv_sqrt(k, ready, done, n):
                pool.wait_ge(ready, n + 1)
                pool.tensor_tensor(rstd[:, k, :], ve[:, k, :], neg_half[:], ALU.pow).then_inc(done, 1)

            def front(s, c):
                inv_sqrt(0, s["ve_ready"], s["pow_done"], c)

            def side(c):
                inv_sqrt(1, ve2_ready, pow2_done, c)

            s = ffn_sems[0]
            front(s, 0)
            front(s, 1)
            step(pool.memset(Vs[:], 0.0))
            pool.memset(Vs[:, :, :, :, HS:HS + 1], 1.0).then_inc(vpads_done, 1)
            pool.wait_ge(vpads_done, 1)
            step(pool.memset(Qs[64:P, :, :, :], 0.0))
            front(s, 2)
            side(0)
            pool.wait_ge(pow2_done, 1)
            step(pool.memset(Ks[64:P, :, :, :], 1.0))
            pool.memset(zrow[:], 0.0).then_inc(pads_done, 1)
            front(s, 3)
            side(1)
            side(2)
            side(3)
            for U in range(NN * NU):
                cc, j = UNITS[U % NU]
                if unit_shape(cc, j)[2]:
                    pool.wait_ge(exp_done, (U + 1) * HQ)
                    v = pr[:, U % NPB, :, 0:P]
                    pool.affine_select(out=v, in_=v, compare_op=ALU.is_ge, fill=0.0, base=0,
                                       pattern=[[0, HQ], [1, P]], channel_multiplier=-1).then_inc(p_masked, 1)
                if U == (NN - 1) * NU + 5:
                    front(ffn_sems[1], 0)
            for c in range(1, NCH):
                front(ffn_sems[1], c)

        @blk.scalar
        def _(act):
            class Ffn:
                def __init__(self, s):
                    self.s = s

                def silu(self, c, f):
                    s, g = self.s, c * NF + f
                    act.wait_ge(s["g_psum"], g + 1)
                    ge(act, s["su_done"], g - 1)
                    act.activation(sg[:, f % 2, :], ps[:, G_BANK, :], ACT.Silu).then_inc(s["sg_ready"], 1)

                def evac_xT(self, c, bank=FRONT_BANK):
                    act.wait_ge(self.s["xT_psum"], c + 1)
                    act.activation(xT[:, c % 2, :], ps[:, bank, :], ACT.Copy).then_inc(self.s["xT_ready"], 1)

                def evac_lgT(self, c, bank=FRONT_BANK):
                    act.wait_ge(self.s["lgT_psum"], c + 1)
                    act.activation(lgT[:], ps[0:NR, bank, :], ACT.Copy).then_inc(self.s["lgT_ready"], 1)

                def tanh(self, c):
                    act.wait_ge(self.s["dz_ready"], c + 1)
                    act.activation(th[:], dz[:], ACT.Tanh, scale=0.5).then_inc(self.s["th_ready"], 1)

                def evac_cT(self, c, bank=FRONT_BANK):
                    act.wait_ge(self.s["cT_psum"], c + 1)
                    act.activation(cT[:, c % 2, :], ps[0:3 * NR, bank, 0:CH // 2].bitcast(BF16), ACT.Copy)\
                        .then_inc(self.s["cT_ready"], 1)

                def evac_y(self, c):
                    act.wait_ge(self.s["h_used"], (c + 1) * NF)
                    ge(act, self.s["yb_psum"], c)
                    act.activation(yT, ps[:, Y_BANK, :], ACT.Copy).then_inc(self.s["yT_ready"], 1)

                def run(self, after):
                    for c in range(NCH):
                        for f in range(NF):
                            self.silu(c, f)
                            if c and f == 2:
                                self.evac_y(c - 1)
                            if c + 1 < NCH:
                                if f == 3:
                                    self.evac_xT(c + 1)
                                if f == 4:
                                    self.evac_lgT(c + 1)
                                if f == 6:
                                    self.tanh(c + 1)
                                if f == 9:
                                    self.evac_cT(c + 1)
                            after(c, f)
                    self.evac_y(NCH - 1)

            def evac_xTa(k):
                act.wait_ge(xTa_psum, k + 1)
                ge(act, v_psum, k)
                act.activation(xTa[:], ps[:, SIDE_BANK, :], ACT.Copy).then_inc(xTa_ready, 1)

            def evac_qk(k, s):
                act.wait_ge(qk_psum, 2 * k + s + 1)
                ge(act, part2_ready, k)
                ge(act, parts_stored, k * 32)
                bias, scale = (bqs[:, 0:1], SCALE) if s == 0 else (bqk[:, 1:2], 1.0)
                act.activation(qf[:, s, :], ps[:, SIDE_BANK, :], ACT.Identity, bias=bias, scale=scale)
                act.activation(qp[:, s, 0, :], ps[:, SIDE_BANK, :], ACT.Identity, bias=bias, scale=scale)\
                    .then_inc(part0_ready, 1)

            def part1(k):
                act.wait_ge(rest_ready, k + 1)
                act.activation(qp[:, :, 1, :], qr, ACT.Copy).then_inc(part1_ready, 1)

            def side0(c, f):
                if f == 8 and c >= 1:
                    evac_xTa(c - 1)
                if f == 9 and c >= 1:
                    evac_qk(c - 1, 0)
                if f == 0 and c >= 2:
                    evac_qk(c - 2, 1)
                if f == 2 and c >= 2:
                    part1(c - 2)

            def evac_o(K):
                N, cc = K // 2, K % 2
                act.wait_ge(pv_done, N * NU + (TC if cc == 0 else NU))
                if K == NN:
                    act.wait_ge(parts_stored, NCH * 32)
                act.activation(oT[:, N // NQ, N % NQ, cc * CH:(cc + 1) * CH], ps[:, O_BANK, :], ACT.Copy)\
                    .then_inc(o_ready, 1)

            def evac_atT(k, bank):
                act.wait_ge(atT_psum, k + 1)
                ge(act, mo_psum, k)
                act.activation(atT[:], ps[:, bank, :], ACT.Copy).then_inc(atT_ready, 1)

            def side1(c, f):
                if f == 7 and c < CB:
                    evac_atT(CB + c, SIDE_BANK)

            act.wait_ge(attn_w_loaded, 8 * 16)
            act.mul(bqs[:], bqk[:, 0:1], SCALE).then_inc(bqs_ready, 1)
            first = Ffn(ffn_sems[0])
            first.evac_xT(0)
            first.evac_lgT(0)
            first.tanh(0)
            first.evac_cT(0)
            act.wait_ge(bqs_ready, 1)
            first.run(side0)
            evac_qk(NCH - 2, 1)
            part1(NCH - 2)
            evac_xTa(NCH - 1)
            evac_qk(NCH - 1, 0)
            evac_qk(NCH - 1, 1)
            part1(NCH - 1)
            second = Ffn(ffn_sems[1])
            for U in range(NN * NU):
                N, u = U // NU, U % NU
                w = unit_shape(*UNITS[u])[1]
                ge(act, pv_done, U - NPB + 1)
                for h in range(HQ):
                    i = U * HQ + h
                    act.wait_ge(st_psum, i + 1)
                    act.activation(pr[:, U % NPB, h, 0:w], ps[:, ST_BANKS[i % 3], 0:w], ACT.Exp).then_inc(exp_done, 1)
                if u == TC:
                    evac_o(2 * N)
                if u == 0 and N:
                    evac_o(2 * N - 1)
                if N == NN - 1:
                    if u == 3:
                        evac_atT(0, A_BANKS[0])
                    if u == 7:
                        second.evac_xT(0, FRONT_BANK2)
                    if u == 8:
                        evac_atT(1, A_BANKS[0])
                    if u == 9:
                        second.evac_lgT(0, FRONT_BANK2)
            second.tanh(0)
            evac_o(2 * NN - 1)
            second.evac_cT(0, FRONT_BANK2)
            second.run(side1)

        @blk.tensor
        def _(pe):
            class Ffn:
                def __init__(self, s):
                    self.s = s

                def turn_x(self, c, bank=FRONT_BANK):
                    pe.wait_ge(self.s["xn_ready"], c + 1)
                    for t in range(TC):
                        ins = pe.transpose(ps[:, bank, t * P:(t + 1) * P], xn[:, 0, t, :], ident[:])
                    ins.then_inc(self.s["xT_psum"], 1)

                def logits(self, c, bank=FRONT_BANK):
                    pe.wait_ge(self.s["xT_ready"], c + 1)
                    pe.matmul(ps[0:NR, bank, :], wr[:], xT[:, c % 2, :], start=True, stop=True)\
                        .then_inc(self.s["lgT_psum"], 1)

                def turn_logits(self, c, bank=FRONT_BANK):
                    pe.wait_ge(self.s["lgT_ready"], c + 1)
                    for t in range(TC):
                        ins = pe.transpose(ps[:, bank, t * NR:(t + 1) * NR], lgT[:, t * P:(t + 1) * P], ident[0:NR, 0:NR])
                    ins.then_inc(self.s["lg_psum"], 1)

                def turn_weights(self, c, bank=FRONT_BANK):
                    pe.wait_ge(self.s["cp_ready"], c + 1)
                    for t in range(TC):
                        ins = pe.transpose(ps[0:3 * NR, bank, 0:CH // 2].bitcast(BF16)[:, t * P:(t + 1) * P],
                                           cp[:, t, :, :].rearrange("p a r -> p (a r)"), identb[:])
                    ins.then_inc(self.s["cT_psum"], 1)

                def up(self, c, f):
                    s, g = self.s, c * NF + f
                    ge(pe, s["sg_ready"], g)
                    pe.matmul(ps[:, G_BANK, :], wg[:, f, :], xT[:, c % 2, :], start=True, stop=True).then_inc(s["g_psum"], 1)
                    ge(pe, s["su_done"], g - 1)
                    pe.matmul(ps[:, U_BANKS[f % 2], :], wu[:, f, :], xT[:, c % 2, :], start=True, stop=True)\
                        .then_inc(s["u_psum"], 1)
                    if f == 0:
                        pe.wait_ge(s["cT_ready"], c + 1)
                    ge(pe, s["h_ready"], g - 1)
                    pe.matmul(ps[:, C_BANKS[f % 2], :], sel[:, f, :], cT[:, c % 2, :], start=True, stop=True)\
                        .then_inc(s["c_psum"], 1)

                def down(self, g):
                    if g < 0:
                        return
                    c, f = divmod(g, NF)
                    pe.wait_ge(self.s["h_ready"], g + 1)
                    if f == 0:
                        ge(pe, self.s["yT_ready"], c)
                    pe.matmul(ps[:, Y_BANK, :], wd[:, f, :], hh[:, f % 2, :], start=f == 0, stop=f == NF - 1)\
                        .then_inc(self.s["h_used"], 1)

                def turn_y(self, c):
                    pe.wait_ge(self.s["yT_ready"], c + 1)
                    for t in range(TC):
                        ins = pe.transpose(ps[:, SIDE_BANK, t * P:(t + 1) * P], yT[:, t * P:(t + 1) * P], ident[:])
                    ins.then_inc(self.s["yb_psum"], 1)

                def run(self, after):
                    for c in range(NCH):
                        for f in range(NF):
                            self.up(c, f)
                            self.down(c * NF + f - 2)
                            if c + 1 < NCH:
                                if f == 2:
                                    self.turn_x(c + 1)
                                if f == 3:
                                    self.logits(c + 1)
                                if f == 4:
                                    self.turn_logits(c + 1)
                                if f == 8:
                                    self.turn_weights(c + 1)
                            after(c, f)
                    self.down(NCH * NF - 2)
                    self.down(NCH * NF - 1)

            first, second = Ffn(ffn_sems[0]), Ffn(ffn_sems[1])

            def turn_xa(k):
                pe.wait_ge(xn2_ready, k + 1)
                for t in range(TC):
                    ins = pe.transpose(ps[:, SIDE_BANK, t * P:(t + 1) * P], xn[:, 1, t, :], ident[:])
                ins.then_inc(xTa_psum, 1)

            def project_qk(k, s):
                if s == 0:
                    pe.wait_ge(xTa_ready, k + 1)
                else:
                    pe.wait_ge(part0_ready, 2 * k + 1)
                pe.matmul(ps[:, SIDE_BANK, :], (wq, wk)[s][:], xTa[:], start=True, stop=True).then_inc(qk_psum, 1)

            def project_v(k):
                pe.wait_ge(part0_ready, 2 * k + 2)
                for t in range(TC):
                    ins = pe.matmul(ps[:, SIDE_BANK, t * P:(t + 1) * P], xTa[:, t * P:(t + 1) * P], wv[:],
                                    start=True, stop=True)
                ins.then_inc(v_psum, 1)

            def side0(c, f):
                if f == 0 and c >= 2:
                    project_v(c - 2)
                if f == 4 and c >= 1:
                    ge(pe, v_ready, c - 1)
                    first.turn_y(c - 1)
                if f == 7 and c >= 1:
                    turn_xa(c - 1)
                if f == 8 and c >= 1:
                    project_qk(c - 1, 0)
                if f == 9 and c >= 1:
                    project_qk(c - 1, 1)

            def a_turn(N, k):
                n, a = N % NQ, N * NTURN + k
                if k == 0:
                    pe.wait_ge(stack_loaded[n], (N // NQ + 1) * 19 * 16)
                ge(pe, a_done, a - len(A_BANKS) + 1)
                bank, turn = A_BANKS[a % len(A_BANKS)], TURNS[k]
                if turn == "max0" or turn == "max1":
                    if turn == "max0":
                        pe.wait_ge(a_done, N * NTURN + LAST_MAX0)
                    else:
                        pe.wait_ge(max1_ready, N + 1)
                    pe.transpose(ps[0:HQ * TC, bank, 0:P],
                                 mmx[:, N % 2, int(turn[3]), :, :].rearrange("p h i -> p (h i)"), ident[:]).then_inc(a_psum, 1)
                    return
                half, h, i, piece = turn
                q = half * CH + i * P
                w = CH if half > piece else (i + 1) * P
                pe.matmul(ps[:, bank, 0:w], Qs[:, n, h, q:q + P], Ks[:, n, h, piece * CH:piece * CH + w],
                          start=True, stop=True).then_inc(a_psum, 1)

            def scores_t(U, h):
                N, (cc, j) = U // NU, UNITS[U % NU]
                n, i = N % NQ, U * HQ + h
                ge(pe, exp_done, i - 2)
                if h == 0 and j == 0:
                    pe.wait_ge(shift_loaded[cc], (N + 1) * 2 * HQ * 16)
                q0, w, _ = unit_shape(cc, j)
                pe.matmul(ps[:, ST_BANKS[i % 3], 0:w], Ks[:, n, h, j * P:(j + 1) * P], Qs[:, n, h, q0:q0 + w],
                          start=True, stop=True).then_inc(st_psum, 1)

            def pv(U):
                N, (cc, j) = U // NU, UNITS[U % NU]
                q0, w, diag = unit_shape(cc, j)
                pe.wait_ge(exp_done, (U + 1) * HQ)
                if diag:
                    pe.wait_ge(p_masked, N * TB + j + 1)
                if j == 0:
                    ge(pe, o_ready, 2 * N + cc)
                for h in range(HQ):
                    ins = pe.matmul(ps[32 * h:32 * h + VC, O_BANK, CH - w:CH], Vs[:, N // NQ, j, (N % NQ) * HQ + h, :],
                                    pr[:, U % NPB, h, 0:w], start=j == 0, stop=j == TC * (cc + 1) - 1,
                                    tile_position=(0, 32 * h))
                ins.then_inc(pv_done, 1)

            def turn_o(k, i, bank):
                for n in range(NQ):
                    t0 = (k % CB) * CH + i * P
                    ins = pe.transpose(ps[:, bank, n * P:(n + 1) * P], oT[:, k // CB, n, t0:t0 + P], ident[:])
                ins.then_inc(ot_psum, 1)

            def turn_at(k, bank):
                pe.wait_ge(at_done, (k + 1) * TC)
                for t in range(TC):
                    ins = pe.transpose(ps[:, bank, t * P:(t + 1) * P], at[:, t, :], ident[:])
                ins.then_inc(atT_psum, 1)

            def project_out(k, bank):
                pe.wait_ge(atT_ready, k + 1)
                for t in range(TC):
                    v = ps[:, bank, t * P:(t + 1) * P]
                    pe.matmul(v, atT[:, t * P:(t + 1) * P], wm[:], start=True, stop=False)
                    ins = pe.matmul(v, ones_row[:], bmr[:], start=False, stop=True)
                ins.then_inc(mo_psum, 1)

            def side1(c, f):
                k = CB + c
                if c < CB:
                    if f < TC:
                        if f == 0:
                            pe.wait_ge(o_ready, 2 * NN)
                            ge(pe, xa_added, k if c else 0)
                        else:
                            pe.wait_ge(at_done, k * TC + f)
                        turn_o(k, f, SIDE_BANK)
                    if f == 6:
                        ge(pe, second.s["y_added"], c)
                        turn_at(k, SIDE_BANK)
                    if f == 8:
                        project_out(k, SIDE_BANK)
                if c and f == 4:
                    if c < CB:
                        pe.wait_ge(at_done, (k + 1) * TC)
                    else:
                        pe.wait_ge(xa_added, NCH)
                    second.turn_y(c - 1)

            pe.wait_ge(const_done, 1)
            first.turn_x(0)
            pe.wait_ge(wr_loaded, 16)
            first.logits(0)
            first.turn_logits(0)
            first.turn_weights(0)
            pe.wait_ge(ffn_w_loaded, 3 * 16)
            pe.wait_ge(attn_w_loaded, 8 * 16)
            first.run(side0)

            for k in range(NTURN - 1):
                a_turn(0, k)
                if k == 1:
                    project_v(NCH - 2)
                if k == 3:
                    pe.wait_ge(v_ready, NCH - 1)
                    first.turn_y(NCH - 1)
                if k == 13:
                    turn_xa(NCH - 1)
                if k == 17:
                    project_qk(NCH - 1, 0)
                if k == 22:
                    project_qk(NCH - 1, 1)
                if k == 27:
                    project_v(NCH - 1)
            pe.wait_ge(v_ready, NCH)
            for U in range(NN * NU):
                N, u = U // NU, U % NU
                for h in range(HQ):
                    scores_t(U, h)
                    if h == 0 and u == 0:
                        a_turn(N, NTURN - 1)
                    if N + 1 < NN:
                        a_turn(N + 1, HQ * u + h)
                        if u == NU - 1 and h == HQ - 1:
                            a_turn(N + 1, NTURN - 2)
                if U:
                    pv(U - 1)
                if N == NN - 1:
                    k = 0 if u < 5 else 1
                    if u in (0, 1, 5, 6):
                        for i in ((0, 1) if u in (0, 5) else (2, 3)):
                            if u == 0 and i == 0:
                                pe.wait_ge(a_done, NN * NTURN)
                            if u == 5 and i == 0:
                                pe.wait_ge(xa_added, 1)
                            turn_o(k, i, A_BANKS[i])
                    if u in (2, 7):
                        turn_at(k, A_BANKS[0])
                    if u in (4, 9):
                        project_out(k, A_BANKS[1])
                    if u == 7:
                        pe.wait_ge(at_done, 2 * TC)
                        second.turn_x(0, FRONT_BANK2)
                    if u == 8:
                        second.logits(0, FRONT_BANK2)
                    if u == 10:
                        second.turn_logits(0, FRONT_BANK2)
            pv(NN * NU - 1)
            second.turn_weights(0, FRONT_BANK2)
            pe.wait_ge(xa_added, 2)
            pe.wait_ge(o_ready, 2 * NN)
            second.run(side1)
            pe.wait_ge(second.s["y_added"], NCH - 1)
            second.turn_y(NCH - 1)

        @blk.vector
        def _(dve):
            steps = [0]

            def step(ins):
                steps[0] += 1
                ins.then_inc(vstep, 1)
                dve.wait_ge(vstep, steps[0])

            def layernorm(k, c, ready, done, xn_ready):
                for t in range(TC):
                    ins = dve.bn_stats(st[:, k, t, :], x[:, c * TC + t, :])
                step(ins)
                for t in range(TC):
                    ins = dve.bn_aggr(mv[:, k, t, :], st[:, k, t, :])
                step(ins)
                dve.tensor_scalar(ve[:, k, :], mv[:, k, :, 1], EPS, None, ALU.add).then_inc(ready, 1)
                dve.wait_ge(done, c + 1)
                for t in range(TC):
                    ins = dve.tensor_scalar(xn[:, k, t, :], x[:, c * TC + t, :], mv[:, k, t, 0:1], rstd[:, k, t:t + 1],
                                            ALU.subtract, ALU.mult)
                ins.then_inc(xn_ready, 1)

            class Ffn:
                def __init__(self, s):
                    self.s = s

                def norm(self, c):
                    ge(dve, self.s["xT_psum"], c)
                    layernorm(0, c, self.s["ve_ready"], self.s["pow_done"], self.s["xn_ready"])

                def route(self, c, bank=FRONT_BANK):
                    s = self.s
                    dve.wait_ge(s["lg_psum"], c + 1)
                    dve.tensor_copy(lg[:], ps[:, bank, 0:TC * NR].rearrange("p (t r) -> p t r", r=NR)).then_inc(s["lg_read"], 1)
                    dve.wait_ge(s["lg_read"], c + 1)
                    for t in range(TC):
                        ins = dve.max(mx8[:, t, :], lg[:, t, 0:E])
                    step(ins)
                    dve.tensor_tensor(dz[:, 0, :], mx8[:, :, 1], mx8[:, :, 0], ALU.subtract)
                    dve.tensor_copy(dz[:, 1, :], lg[:, :, E]).then_inc(s["dz_ready"], 1)
                    for t in range(TC):
                        ins = dve.max_index(ix8[:, t, :], mx8[:, t, :], lg[:, t, 0:E])
                    step(ins)
                    step(dve.tensor_copy(ixf[:], ix8[:, :, 0:2]))
                    experts = iota_e[:].unsqueeze(1).broadcast_to([P, TC, E])
                    dve.tensor_tensor(e1[:], experts, ixf[:, :, 0:1].broadcast_to([P, TC, E]), ALU.is_equal)
                    step(dve.tensor_tensor(e2[:], experts, ixf[:, :, 1:2].broadcast_to([P, TC, E]), ALU.is_equal))

                def weigh(self, c):
                    s = self.s
                    dve.wait_ge(s["th_ready"], c + 1)
                    step(dve.tensor_scalar(rw[:, 0:2, :], th[:], 1.0, 0.25, ALU.add, ALU.mult))
                    dve.tensor_copy(cf[:, :, E], rw[:, 1, :])
                    step(dve.tensor_scalar(rw[:, 2, :], rw[:, 0, :], -1.0, 0.5, ALU.mult, ALU.add))
                    dve.tensor_tensor(e1[:], e1[:], rw[:, 2, :].unsqueeze(2).broadcast_to([P, TC, E]), ALU.mult)
                    step(dve.tensor_tensor(e2[:], e2[:], rw[:, 0, :].unsqueeze(2).broadcast_to([P, TC, E]), ALU.mult))
                    step(dve.tensor_tensor(cf[:, :, 0:E], e1[:], e2[:], ALU.add))
                    ge(dve, s["cT_psum"], c)
                    step(dve.tensor_copy(cp[:, :, 0, :], cf[:]))
                    step(dve.tensor_tensor(cr[:], cf[:], cp[:, :, 0, :], ALU.subtract))
                    step(dve.tensor_copy(cp[:, :, 1, :], cr[:]))
                    dve.tensor_tensor(cp[:, :, 2, :], cr[:], cp[:, :, 1, :], ALU.subtract).then_inc(s["cp_ready"], 1)

                def times_u(self, g):
                    s, f = self.s, g % NF
                    dve.wait_ge(s["sg_ready"], g + 1)
                    dve.wait_ge(s["u_psum"], g + 1)
                    ge(dve, s["h_ready"], g - 2)
                    dve.tensor_tensor(su[:, g % 3, :], ps[:, U_BANKS[f % 2], :], sg[:, f % 2, :], ALU.mult).then_inc(s["su_done"], 1)

                def times_c(self, g):
                    if g < 0:
                        return
                    s, f = self.s, g % NF
                    dve.wait_ge(s["su_done"], g + 1)
                    dve.wait_ge(s["c_psum"], g + 1)
                    ge(dve, s["h_used"], g - 1)
                    dve.tensor_tensor(hh[:, f % 2, :], ps[:, C_BANKS[f % 2], :], su[:, g % 3, :], ALU.mult).then_inc(s["h_ready"], 1)

                def add_y(self, c):
                    dve.wait_ge(self.s["yb_psum"], c + 1)
                    dve.tensor_tensor(xs(c), ps[:, SIDE_BANK, :].rearrange("p (t d) -> p t d", d=D), xs(c), ALU.add)\
                        .then_inc(self.s["y_added"], 1)

                def run(self, after):
                    for c in range(NCH):
                        for f in range(NF):
                            self.times_u(c * NF + f)
                            self.times_c(c * NF + f - 1)
                            if c and f == 5:
                                self.add_y(c - 1)
                            if c + 1 < NCH:
                                if f == 1:
                                    self.norm(c + 1)
                                if f == 5:
                                    self.route(c + 1)
                                if f == 7:
                                    self.weigh(c + 1)
                            after(c, f)
                    self.times_c(NCH * NF - 1)

            first, second = Ffn(ffn_sems[0]), Ffn(ffn_sems[1])

            def norm_a(k):
                dve.wait_ge(first.s["y_added"], k + 1)
                ge(dve, xTa_psum, k)
                layernorm(1, k, ve2_ready, pow2_done, xn2_ready)

            def rest(k):
                dve.wait_ge(part0_ready, 2 * k + 2)
                dve.tensor_tensor(qr, qf, qp[:, :, 0, :], ALU.subtract).then_inc(rest_ready, 1)

            def add_v(k):
                dve.wait_ge(v_psum, k + 1)
                j = (k % CB) * TC
                if k == 0:
                    dve.wait_ge(vpads_done, 1)
                dve.tensor_tensor(Vs[:, k // CB, j:j + TC, :, 0:HS],
                                  ps[:, SIDE_BANK, :].rearrange("p (t h d) -> p t h d", h=H, d=HS),
                                  bvb[:].rearrange("p (h d) -> p h d", d=HS).unsqueeze(1).broadcast_to([P, TC, H, HS]),
                                  ALU.add).then_inc(v_ready, 1)

            def part2(k):
                dve.wait_ge(part1_ready, k + 1)
                dve.tensor_tensor(qp[:, :, 2, :], qr, qp[:, :, 1, :], ALU.subtract).then_inc(part2_ready, 1)

            def side0(c, f):
                if f == 6 and c >= 1:
                    norm_a(c - 1)
                if f == 1 and c >= 2:
                    rest(c - 2)
                    add_v(c - 2)
                if f == 3 and c >= 2:
                    part2(c - 2)

            def a_turn(N, k):
                a = N * NTURN + k
                dve.wait_ge(a_psum, a + 1)
                b4 = a % len(A_BANKS)
                bank, turn = A_BANKS[b4], TURNS[k]
                if turn == "max0" or turn == "max1":
                    half = int(turn[3])
                    ge(dve, shift_loaded[half], N * 2 * HQ * 16)
                    step(dve.tensor_scalar(srow[:, half, 0, :], ps[0:HQ * TC, bank, 0:P], -1.0, None, ALU.mult))
                    dve.scalar_tensor_tensor(out=srow[:, half, 1, :], in0=ps[0:HQ * TC, bank, 0:P], scalar=-1.0,
                                             in1=srow[:, half, 0, :], op0=ALU.mult, op1=ALU.subtract).then_inc(a_done, 1)
                    return
                half, h, i, piece = turn
                dst = m2[:, N % 2, h, i, piece:piece + 1] if half else mmx[:, N % 2, 0, h, i:i + 1]
                if half > piece:
                    dve.reduce_max(dst, ps[:, bank, :], AX.X).then_inc(a_done, 1)
                else:
                    w = (i + 1) * P
                    dve.tensor_tensor_reduce(out=junk[:, b4, 0:w], in0=ps[:, bank, 0:w], in1=mask[:, CH - w:CH], scale=1.0,
                                             scalar=-3e38, op0=ALU.add, op1=ALU.max, accum_out=dst).then_inc(a_done, 1)
                if k == NTURN - 2:
                    dve.wait_ge(a_done, a + 1)
                    dve.tensor_tensor(mmx[:, N % 2, 1, :, :], m2[:, N % 2, :, :, 0], m2[:, N % 2, :, :, 1],
                                      ALU.max).then_inc(max1_ready, 1)

            def normalise(k, i, bank):
                dve.wait_ge(ot_psum, k * TC + i + 1)
                heads = ps[:, bank, :].rearrange("p (h v) -> p h v", v=32)
                step(dve.reciprocal(rec[:, i, :], heads[:, :, HS]))
                if i == 0:
                    ge(dve, atT_psum, k)
                dve.tensor_tensor(at[:, i, :].rearrange("p (h d) -> p h d", d=HS), heads[:, :, 0:HS],
                                  rec[:, i, :].unsqueeze(2).broadcast_to([P, H, HS]), ALU.mult).then_inc(at_done, 1)

            def add_out(k, bank):
                dve.wait_ge(mo_psum, k + 1)
                dve.tensor_tensor(xs(k), ps[:, bank, :].rearrange("p (t d) -> p t d", d=D), xs(k), ALU.add).then_inc(xa_added, 1)

            def side1(c, f):
                if c < CB:
                    if 1 <= f <= TC:
                        normalise(CB + c, f - 1, SIDE_BANK)
                    if f == 9:
                        add_out(CB + c, SIDE_BANK)
                        dve.wait_ge(xa_added, CB + c + 1)

            dve.wait_ge(x_first_loaded, 16)
            first.norm(0)
            dve.wait_ge(const_done, 1)
            first.route(0)
            first.weigh(0)
            dve.wait_ge(x_rest_loaded, 16)
            dve.wait_ge(attn_w_loaded, 8 * 16)
            first.run(side0)
            for k in range(NTURN - 1):
                a_turn(0, k)
                if k == 1:
                    rest(NCH - 2)
                    add_v(NCH - 2)
                if k == 3:
                    first.add_y(NCH - 1)
                    norm_a(NCH - 1)
                if k == 5:
                    part2(NCH - 2)
                if k == 24:
                    rest(NCH - 1)
                if k == 27:
                    add_v(NCH - 1)
                if k == 30:
                    part2(NCH - 1)
            for N in range(NN):
                a_turn(N, NTURN - 1)
                if N + 1 < NN:
                    for k in range(NTURN - 1):
                        a_turn(N + 1, k)
            for i in range(TC):
                normalise(0, i, A_BANKS[i])
            add_out(0, A_BANKS[1])
            dve.wait_ge(xa_added, 1)
            for i in range(TC):
                normalise(1, i, A_BANKS[i])
            second.norm(0)
            add_out(1, A_BANKS[1])
            dve.wait_ge(xa_added, 2)
            second.route(0, FRONT_BANK2)
            second.weigh(0)
            second.run(side1)
            second.add_y(NCH - 1)


_OUT = ("out_dram", (B, S, D))


def kernel(**inputs):
    import numpy as np
    import concourse.bacc as bacc
    from concourse.bass_utils import run_bass_kernel_spmd

    a = {k.removeprefix("L0_"): np.asarray(v) for k, v in inputs.items()}
    hid = lambda e, s: np.concatenate([e.reshape(E * MH, D), s], 0).T
    arrays = {
        "x": a["attn_x"].reshape(T, D),
        "w_gate": hid(a["ffn_We_gate"], a["ffn_Ws_gate"]),
        "w_up": hid(a["ffn_We_up"], a["ffn_Ws_up"]),
        "w_down": np.concatenate([a["ffn_We_down"].transpose(0, 2, 1).reshape(E * MH, D), a["ffn_Ws_down"].T], 0),
        "w_route": np.concatenate([a["ffn_Wg"], a["ffn_Wsg"]], 0).T,
    }
    for n in ("Wq", "bq", "Wk", "bk", "Wv", "bv", "Wm", "bm"):
        arrays[n] = a["attn_" + n]
    arrays = {f"in_{n}": np.ascontiguousarray(v) for n, v in arrays.items()}
    nc = bacc.Bacc("TRN2", target_bir_lowering=False, num_devices=1)
    args = [nc.dram_tensor(n, v.shape, mybir.dt.from_np(v.dtype), kind="ExternalInput").ap() for n, v in arrays.items()]
    args.append(nc.dram_tensor(_OUT[0], (T, D), F32, kind="ExternalOutput").ap())
    macaron(nc, *args)
    r = run_bass_kernel_spmd(nc, [arrays], core_ids=[0])
    return r.results[0][_OUT[0]].reshape(_OUT[1])
```

```python
import concourse.bass as bass
from concourse import mybir
from contextlib import ExitStack

F32 = mybir.dt.float32
F32R = mybir.dt.float32r
BF16 = mybir.dt.bfloat16
U32 = mybir.dt.uint32
ALU = mybir.AluOpType
ACT = mybir.ActivationFunctionType
AX = mybir.AxisListType

P = 128
D = 128
B, S = 2, 1024
T = B * S
NT = T // P
CH = 512
TC = CH // P
NCH = T // CH
E, MH, SH = 16, 64, 256
EH = E * MH + SH
NF = EH // P
NR = E + 1
H, HS = 16, 8
SCALE = HS ** -0.5
NQ = 4
HQ = H // NQ
TB = S // P
CB = S // CH
ROWS = 9 * HS
SHIFT = ROWS
VC = HS + 1
EPS = 1e-5
BIG = -1e30

HALF0 = [(0, h, i, 0) for i in range(TC) for h in range(HQ)]
HALF1 = [(1, h, i, p) for i in range(TC) for h in range(HQ) for p in range(2)]
OLD = 5
TURNS = HALF0[:OLD] + ["max1"] + HALF0[OLD:] + HALF1[:2] + ["max0"] + HALF1[2:]
NTURN = len(TURNS)
UNITS = [(cc, j) for cc in range(CB) for j in range(TC * (cc + 1))]
NU = len(UNITS)
NN = B * NQ


def unit_shape(cc, j):
    q0 = max(CH * cc, P * j)
    return q0, CH * (cc + 1) - q0, P * j >= CH * cc


def turn_no(N, k):
    if N == NN:
        return NN * NTURN - 1
    return N * NTURN + k - (1 if N or k > OLD else 0)


def turns_at():
    def cost(turn):
        half, h, i, piece = (0, 0, 0, 0) if isinstance(turn, str) else turn
        return 150 + (CH if half > piece else (i + 1) * P)
    slots = [(u, h) for u in range(NU) for h in range(HQ)]
    share = [unit_shape(*UNITS[u])[1] + 100 for u, h in slots]
    total, all_turns = sum(share), sum(map(cost, TURNS))
    at, k, spent, time = {}, 0, 0, 0
    for slot, w in zip(slots, share):
        at[slot] = []
        time += w
        while k < NTURN and (spent + cost(TURNS[k]) / 2) * total <= time * all_turns:
            at[slot].append(k)
            spent += cost(TURNS[k])
            k += 1
    at[slots[-1]] += range(k, NTURN)
    return at


TURNS_AT = turns_at()
EARLY = TURNS.index("max0")
NPB = 3
NLAST = ((NN - 1) * NU + 1) * HQ

G_BANK, U_BANKS, C_BANK, EXTRA_BANK, Y_BANK, FRONT_BANK, SIDE_BANK = 0, (1, 2), 3, 4, 5, 6, 7
O_BANK, A_BANKS, ST_BANKS = 0, (1, 2, 3, 4), (5, 6, 7)
LAST_BANKS = (4, 6, 7, 5)
PROJ_BANKS = (1, 2, 3)
FRONT_BANK2 = 3
EARLY_KS = [k for k in range(EARLY) if k != OLD]
EARLY_TURNS = len(EARLY_KS)


def early_at():
    blocks = [(NCH - 2, 9)] + [(NCH - 1, f) for f in (0, 1, 2, 3, 4, 7, 8, 9)]
    return {(b, half): EARLY_KS[2 * i + half] for i, b in enumerate(blocks) for half in range(2)}


EARLY_AT = early_at()
TWO_FROM = 2 * 3
SECOND_Y = {(CB, 0): 0, (CB, 4): 1, (NCH - 1, 4): 2}


def c_bank(use, g):
    extra_free = g // NF < CB if use == 0 else g // NF >= CB
    return EXTRA_BANK if extra_free and g % 2 else C_BANK


def st_bank(i):
    return ST_BANKS[i % len(ST_BANKS)] if i < NLAST else LAST_BANKS[(i - NLAST) % len(LAST_BANKS)]


def bank_of(a):
    if a < EARLY_TURNS:
        return FRONT_BANK if a > TWO_FROM and a % 2 else EXTRA_BANK
    return A_BANKS[a % len(A_BANKS)]


def turns_before(a):
    if a < EARLY_TURNS:
        return a - 1 if a > TWO_FROM else a
    return max(EARLY_TURNS, a - len(A_BANKS) + 1)


def macaron(nc, x_in, w_gate, w_up, w_down, w_route, Wq, bq, Wk, bk, Wv, bv, Wm, bm, out):
    ctx = ExitStack()
    with ctx:
        def sb(name, shape, dt=F32):
            return ctx.enter_context(nc.sbuf_tensor(name, shape, dt))

        def sem(name):
            return ctx.enter_context(nc.semaphore(name))

        x = sb("x", [P, NT, D])
        wgh = sb("wgh", [P, NF, P], F32R)
        wgl = sb("wgl", [P, NF, P], F32R)
        wuh = sb("wuh", [P, NF, P], F32R)
        wul = sb("wul", [P, NF, P], F32R)
        wrh = sb("wrh", [P, NR], F32R)
        wrl = sb("wrl", [P, NR], F32R)
        wdh = sb("wdh", [P, NF, D], F32R)
        wdl = sb("wdl", [P, NF, D], F32R)
        wq = sb("wq", [P, P])
        wk = sb("wk", [P, P])
        wv = sb("wv", [P, P])
        wm = sb("wm", [P, P])
        bqk = sb("bqk", [P, 2])
        bqs = sb("bqs", [P, 1])
        bvc = sb("bvc", [P, 1])
        bmb = sb("bmb", [P, P])
        ident = sb("ident", [P, P])
        identb = sb("identb", [P, P], BF16)
        sel = sb("sel", [3 * NR, NF, P], BF16)
        iota_e = sb("iota_e", [P, E])
        neg_half = sb("neg_half", [P, TC])
        mask = sb("mask", [P, CH], BF16)
        st = sb("st", [P, 2, TC, 6])
        mv = sb("mv", [P, 2, TC, 2])
        ve = sb("ve", [P, 2, TC])
        rstd = sb("rstd", [P, 2, TC])
        xn = sb("xn", [P, 2, TC, D])
        xTh = sb("xTh", [P, 2, CH], F32R)
        xTl = sb("xTl", [P, 2, CH], F32R)
        xTa = sb("xTa", [P, CH])
        lgT = sb("lgT", [NR, CH])
        lg = sb("lg", [P, TC, NR])
        mx8 = sb("mx8", [P, TC, 8])
        ix8 = sb("ix8", [P, TC, 8], U32)
        ixf = sb("ixf", [P, TC, 2])
        dz = sb("dz", [P, 2, TC])
        th = sb("th", [P, 2, TC])
        rw = sb("rw", [P, 3, TC])
        e1 = sb("e1", [P, TC, E])
        e2 = sb("e2", [P, TC, E])
        cf = sb("cf", [P, TC, NR])
        cr = sb("cr", [P, TC, NR])
        cp = sb("cp", [P, TC, 3, NR], BF16)
        cT = sb("cT", [3 * NR, 2, CH], BF16)
        Qs = sb("Qs", [P, NQ, CB, HQ, CH], BF16)
        Ks = sb("Ks", [P, NQ, CB, HQ, CH], BF16)
        pads = sb("pads", [P - ROWS, 2, CH], BF16)
        Vs = sb("Vs", [P, B, TB, H, VC])
        mmx = sb("mmx", [P, 2, 2, HQ, TC])
        m2 = sb("m2", [P, 2, HQ, TC, 2])
        srow = sb("srow", [HQ * TC, 2, 2, P], BF16)
        oT = sb("oT", [P, B, NQ, S])
        rec = sb("rec", [P, TC, H])
        at, atT = xn[:, 1, :, :], xTa
        pr = sb("pr", [P, NPB, HQ, CH])
        hh = sb("hh", [P, 2, CH], F32R)
        hl = sb("hl", [P, 2, CH], F32R)
        hid = pr[:].rearrange("p b h t -> p (b h) t")
        sg, su, hid_h, yT = hid[:, 0:2, :], hid[:, 2:5, :], hid[:, 5:7, :], hid[:, 7, :]
        spare0 = oT[:, 0, :, :].rearrange("p n t -> p (n t)")
        wg_in = spare0[:, 0:EH].rearrange("p (f q) -> p f q", q=P)
        wu_in = spare0[:, EH:2 * EH].rearrange("p (f q) -> p f q", q=P)
        wd_in = spare0[:, 2 * EH:3 * EH].rearrange("p (f d) -> p f d", d=D)
        wr_in = spare0[:, 3 * EH:3 * EH + NR]
        spare = [oT[:, 1 - b, :, :].rearrange("p n t -> p (n t)") for b in range(2)]
        qf = [v[:, 0:2 * CH].rearrange("p (s t) -> p s t", s=2) for v in spare]
        qr = [v[:, 2 * CH:4 * CH].rearrange("p (s t) -> p s t", s=2) for v in spare]
        qp = [v[:, 4 * CH:7 * CH].bitcast(BF16).rearrange("p (s a t) -> p s a t", s=2, a=3) for v in spare]

        ps = ctx.enter_context(nc.psum_tensor("ps", [P, 8, CH], F32))
        parts = nc.dram_tensor("parts", [B, CB, NQ, 2, 3, HS, HQ, CH], BF16, kind="Internal").ap()
        out_v = out.rearrange("(n p) d -> p n d", p=P)

        x_first_loaded = sem("x_first_loaded")
        x_rest_loaded = sem("x_rest_loaded")
        wr_loaded = sem("wr_loaded")
        wg_loaded, wu_loaded, wd_loaded = sem("wg_loaded"), sem("wu_loaded"), sem("wd_loaded")
        high_parts = sem("high_parts")
        wrl_ready = sem("wrl_ready")
        low_parts = sem("low_parts")
        wdl_ready = sem("wdl_ready")
        attn_w_loaded = sem("attn_w_loaded")
        const_step = sem("const_step")
        ident_done, iota_done, sel_done = sem("ident_done"), sem("iota_done"), sem("sel_done")
        pads_done = sem("pads_done")
        pads_loaded = sem("pads_loaded")
        vpads_done = sem("vpads_done")
        mask_done = sem("mask_done")
        vstep = sem("vstep")
        out_stored = sem("out_stored")
        FFN_SEMS = ("ve_ready", "pow_done", "xn_ready", "xT_psum", "xTh_ready", "xTl_ready", "lgT_psum", "lgT_ready",
                    "lg_psum", "lg_read", "dz_ready", "th_ready", "cp_ready", "cT_psum", "cT_ready",
                    "g_psum", "u_psum", "c_psum", "sg_ready", "su_done", "h_ready", "hh_ready", "hl_ready",
                    "h_used",
                    "yT_ready", "yb_psum", "y_added")
        ffn_sems = [{n: sem(f"{n}{k}") for n in FFN_SEMS} for k in range(2)]
        bqs_ready = sem("bqs_ready")
        ve2_ready, pow2_done, xn2_ready = sem("ve2_ready"), sem("pow2_done"), sem("xn2_ready")
        xTa_psum, xTa_ready = sem("xTa_psum"), sem("xTa_ready")
        qk_psum, v_psum = sem("qk_psum"), sem("v_psum")
        qf_ready, part0_ready = sem("qf_ready"), sem("part0_ready")
        rest_ready = sem("rest_ready")
        part1_ready, part2_ready = sem("part1_ready"), sem("part2_ready")
        v_ready = sem("v_ready")
        parts_stored = sem("parts_stored")
        stack_loaded = [sem(f"stack_loaded{n}") for n in range(NQ)]
        shift_loaded = [sem(f"shift_loaded{h}") for h in range(2)]
        a_psum, a_done, max1_ready = sem("a_psum"), sem("a_done"), sem("max1_ready")
        st_psum, exp_done, p_masked, pv_done = sem("st_psum"), sem("exp_done"), sem("p_masked"), sem("pv_done")
        o_ready = sem("o_ready")
        ot_psum, at_done = sem("ot_psum"), sem("at_done")
        atT_psum, atT_ready = sem("atT_psum"), sem("atT_ready")
        mo_psum, xa_added = sem("mo_psum"), sem("xa_added")

        blk = ctx.enter_context(nc.Block())

        def ge(eng, s, v):
            if v > 0:
                eng.wait_ge(s, v)

        def xs(c):
            return x[:, c * TC:(c + 1) * TC, :]

        @blk.sync
        def _(sp):
            x_v = x_in.rearrange("(n p) d -> p n d", p=P)
            sp.dma_start(x[:, 0:TC, :], x_v[:, 0:TC, :]).then_inc(x_first_loaded, 16)
            sp.dma_start(wr_in, w_route).then_inc(wr_loaded, 16)
            sp.dma_start(wg_in, w_gate.rearrange("d (f p) -> d f p", p=P)).then_inc(wg_loaded, 16)
            sp.dma_start(wu_in, w_up.rearrange("d (f p) -> d f p", p=P)).then_inc(wu_loaded, 16)
            sp.dma_start(wd_in, w_down.rearrange("(f p) d -> p f d", p=P)).then_inc(wd_loaded, 16)
            sp.dma_start(x[:, TC:, :], x_v[:, TC:, :]).then_inc(x_rest_loaded, 16)
            for w, src in ((wq, Wq), (wk, Wk), (wv, Wv), (wm, Wm)):
                sp.dma_start(w[:], src).then_inc(attn_w_loaded, 16)
            sp.dma_start(bqk[:, 0:1], bq.rearrange("(p a) -> p a", a=1)).then_inc(attn_w_loaded, 16)
            sp.dma_start(bqk[:, 1:2], bk.rearrange("(p a) -> p a", a=1)).then_inc(attn_w_loaded, 16)
            sp.dma_start(bvc[:], bv.rearrange("(p a) -> p a", a=1)).then_inc(attn_w_loaded, 16)
            sp.dma_start(bmb[:], bm.rearrange("(a p) -> a p", a=1).broadcast_to([P, P])).then_inc(attn_w_loaded, 16)

            sp.wait_ge(pads_done, 1)
            for stack, value in ((Qs, 0), (Ks, 1)):
                sp.dma_start(stack[ROWS:P, :, :, :, :].rearrange("r n c h t -> r (n c h) t"),
                             pads[:, value, :].unsqueeze(1).broadcast_to([P - ROWS, NQ * CB * HQ, CH])).then_inc(pads_loaded, 16)

            def store_parts(k):
                sp.wait_ge(part2_ready, k + 1)
                for n in range(NQ):
                    sp.dma_start(parts[k // CB, k % CB, n, :, :, :, :, :].rearrange("s a d h t -> (d h) (s a) t"),
                                 qp[k % 2][n * HQ * HS:(n + 1) * HQ * HS, :, :, :].rearrange("p s a t -> p (s a) t"))\
                        .then_inc(parts_stored, 16)

            def load_stack(b, n, chunks):
                for c in chunks:
                    def stacked(w, a0, a1):
                        return parts[b, c, n, w, a0:a1, :, :, :].rearrange("a d h t -> (a d) (h t)")

                    sp.dma_start(Ks[0:ROWS, n, c, :, :].rearrange("r h t -> r (h t)"),
                                 stacked(1, 0, 3).unsqueeze(0).broadcast_to([3, 3 * HS, HQ * CH])).then_inc(stack_loaded[n], 16)
                    for a in range(3):
                        sp.dma_start(Qs[a * 3 * HS:(a + 1) * 3 * HS, n, c, :, :].rearrange("r h t -> r (h t)"),
                                     stacked(0, a, a + 1).unsqueeze(0).broadcast_to([3, HS, HQ * CH])).then_inc(stack_loaded[n], 16)
                    if b and c == 0:
                        sp.dma_start(Qs[SHIFT:SHIFT + 2, n, :, :, :].rearrange("a c h t -> a (c h) t"),
                                     pads[0:2, 0, :].unsqueeze(1).broadcast_to([2, CB * HQ, CH])).then_inc(stack_loaded[n], 16)

            def load_shift(N, half):
                sp.wait_ge(a_done, (turn_no(N, TURNS.index("max0")) if half == 0 else turn_no(N + 1, OLD)) + 1)
                for part in range(2):
                    sp.dma_start(Qs[SHIFT + part:SHIFT + part + 1, N % NQ, half, :, :].rearrange("a h t -> a (h t)"),
                                 srow[:, half, part, :]).then_inc(shift_loaded[half], 16)

            store_parts(0)
            sp.wait_ge(parts_stored, NQ * 16)
            load_stack(0, 0, (0,))
            store_parts(1)
            sp.wait_ge(parts_stored, CB * NQ * 16)
            load_stack(0, 0, (1,))
            load_stack(0, 1, range(CB))
            load_shift(0, 0)
            store_parts(CB)
            load_stack(0, 2, range(CB))
            load_stack(0, 3, range(CB))
            load_shift(0, 1)
            store_parts(CB + 1)
            sp.wait_ge(parts_stored, NCH * NQ * 16)
            for N in range(NN):
                if N:
                    load_shift(N, 1)
                if 1 <= N <= NQ:
                    sp.wait_ge(pv_done, N * NU)
                    load_stack(1, N - 1, range(CB))
                if N + 1 < NN:
                    load_shift(N + 1, 0)
            for c in range(NCH):
                sp.wait_ge(ffn_sems[1]["y_added"], c + 1)
                sp.dma_start(out_v[:, c * TC:(c + 1) * TC, :], xs(c)).then_inc(out_stored, 16)
            sp.wait_ge(out_stored, NCH * 16)

        @blk.gpsimd
        def _(pool):
            done = [0]

            def step(ins):
                done[0] += 1
                ins.then_inc(const_step, 1)
                pool.wait_ge(const_step, done[0])

            def inv_sqrt(k, ready, done, n):
                pool.wait_ge(ready, n + 1)
                pool.tensor_tensor(rstd[:, k, :], ve[:, k, :], neg_half[:], ALU.pow).then_inc(done, 1)

            def front(s, c):
                inv_sqrt(0, s["ve_ready"], s["pow_done"], c)

            def side(c):
                inv_sqrt(1, ve2_ready, pow2_done, c)

            pool.memset(neg_half[:], -0.5)
            step(pool.memset(ident[:], 0.0))
            pool.affine_select(out=ident[:], in_=ident[:], compare_op=ALU.not_equal, fill=1.0, base=0,
                               pattern=[[-1, P]], channel_multiplier=1).then_inc(ident_done, 1)
            s = ffn_sems[0]
            front(s, 0)
            pool.iota(iota_e[:], pattern=[[1, E]], base=0, channel_multiplier=0, allow_small_or_imprecise_dtypes=True)\
                .then_inc(iota_done, 1)
            pool.memset(pads[:, 0, :], 0.0)
            pool.memset(pads[:, 1, :], 1.0).then_inc(pads_done, 1)
            step(pool.memset(sel[:], 0.0))
            routed = sel[:, 0:E * MH // P, :].rearrange("r f (s m) -> r f s m", m=MH)
            shared = sel[:, E * MH // P:NF, :]
            for part in range(3):
                pool.affine_select(out=routed, in_=routed, compare_op=ALU.not_equal, fill=1.0, base=-NR * part,
                                   pattern=[[-P // MH, E * MH // P], [-1, P // MH], [0, MH]], channel_multiplier=1)
                step(pool.affine_select(out=shared, in_=shared, compare_op=ALU.not_equal, fill=1.0,
                                        base=-NR * part - E, pattern=[[0, SH // P], [0, P]], channel_multiplier=1))
            pool.tensor_copy(identb[:], ident[:]).then_inc(sel_done, 1)
            pool.wait_ge(high_parts, 4)
            pool.tensor_tensor(wdl[:], wd_in, wdh[:].bitcast(F32), ALU.subtract).then_inc(wdl_ready, 1)

            def low_h(s, g):
                if g < 0:
                    return
                pool.wait_ge(s["hh_ready"], g + 1)
                pool.tensor_tensor(hl[:, g % 2, :], hid_h[:, g % 2, :], hh[:, g % 2, :].bitcast(F32), ALU.subtract)\
                    .then_inc(s["hl_ready"], 1)

            def rest(k):
                pool.wait_ge(part0_ready, 2 * k + 2)
                pool.tensor_tensor(qr[k % 2], qf[k % 2], qp[k % 2][:, :, 0, :], ALU.subtract).then_inc(rest_ready, 1)

            def part2(k):
                pool.wait_ge(part1_ready, k + 1)
                pool.tensor_tensor(qp[k % 2][:, :, 2, :], qr[k % 2], qp[k % 2][:, :, 1, :], ALU.subtract).then_inc(part2_ready, 1)

            for c in range(NCH):
                for f in range(NF):
                    if c and f == 6:
                        side(c - 1)
                    low_h(s, c * NF + f - 2)
                    if f == 0 and c + 1 < NCH:
                        front(s, c + 1)
                    if c == 0 and f == 3:
                        pool.memset(Vs[:], 1.0).then_inc(vpads_done, 1)
                    if c == 0 and f == 6:
                        step(pool.memset(mask[:], 0.0))
                        last = mask[:, CH - P:CH]
                        pool.affine_select(out=last, in_=last, compare_op=ALU.is_ge, fill=BIG, base=0,
                                           pattern=[[-1, P]], channel_multiplier=1).then_inc(mask_done, 1)
            low_h(s, NCH * NF - 2)
            low_h(s, NCH * NF - 1)

            side(NCH - 1)
            rest(NCH - 2)
            part2(NCH - 2)
            rest(NCH - 1)
            part2(NCH - 1)
            for U in range(NN * NU):
                cc, j = UNITS[U % NU]
                if unit_shape(cc, j)[2]:
                    pool.wait_ge(exp_done, (U + 1) * HQ)
                    v = pr[:, U % NPB, :, 0:P]
                    pool.affine_select(out=v, in_=v, compare_op=ALU.is_ge, fill=0.0, base=0,
                                       pattern=[[0, HQ], [1, P]], channel_multiplier=-1).then_inc(p_masked, 1)
                if U == (NN - 1) * NU + 4:
                    front(ffn_sems[1], 0)
            s = ffn_sems[1]
            for c in range(NCH):
                for f in range(NF):
                    if f == 0 and c + 1 < NCH:
                        front(s, c + 1)
                    low_h(s, c * NF + f - 2)
            low_h(s, NCH * NF - 2)
            low_h(s, NCH * NF - 1)

        @blk.scalar
        def _(act):
            class Ffn:
                def __init__(self, s):
                    self.s, self.use = s, ffn_sems.index(s)

                def silu(self, c, f):
                    s, g = self.s, c * NF + f
                    act.wait_ge(s["g_psum"], g + 1)
                    ge(act, s["su_done"], g - 1)
                    act.activation(sg[:, f % 2, :], ps[:, G_BANK, :], ACT.Silu).then_inc(s["sg_ready"], 1)

                def evac_xT(self, c, bank=FRONT_BANK):
                    act.wait_ge(self.s["xT_psum"], c + 1)
                    act.activation(xTh[:, c % 2, :], ps[:, bank, :], ACT.Copy).then_inc(self.s["xTh_ready"], 1)

                def evac_lgT(self, c, bank=FRONT_BANK):
                    act.wait_ge(self.s["lgT_psum"], c + 1)
                    act.activation(lgT[:], ps[0:NR, bank, :], ACT.Copy).then_inc(self.s["lgT_ready"], 1)

                def tanh(self, c):
                    act.wait_ge(self.s["dz_ready"], c + 1)
                    act.activation(th[:], dz[:], ACT.Tanh, scale=0.5).then_inc(self.s["th_ready"], 1)

                def evac_cT(self, c, bank=FRONT_BANK):
                    act.wait_ge(self.s["cT_psum"], c + 1)
                    act.activation(cT[:, c % 2, :], ps[0:3 * NR, bank, 0:CH // 2].bitcast(BF16), ACT.Copy)\
                        .then_inc(self.s["cT_ready"], 1)

                def high_h(self, g):
                    if g < 0:
                        return
                    act.wait_ge(self.s["h_ready"], g + 1)
                    ge(act, self.s["h_used"], g - 1)
                    act.activation(hh[:, g % 2, :], hid_h[:, g % 2, :], ACT.Copy).then_inc(self.s["hh_ready"], 1)

                def evac_y(self, c):
                    act.wait_ge(self.s["h_used"], (c + 1) * NF)
                    ge(act, self.s["yb_psum"], c)
                    act.activation(yT, ps[:, Y_BANK, :], ACT.Copy).then_inc(self.s["yT_ready"], 1)

                def run(self, before, after, weights_out=False):
                    for c in range(NCH):
                        for f in range(NF):
                            if c and f == 3:
                                self.evac_y(c - 1)
                            if c + 1 < NCH:
                                if f == 3:
                                    self.evac_xT(c + 1)
                                if f == 5:
                                    self.evac_lgT(c + 1)
                            before(c, f)
                            if c or f:
                                self.silu(c, f)
                            if f == 1 and (c or not weights_out):
                                self.evac_cT(c)
                            self.high_h(c * NF + f - 2)
                            after(c, f)
                            if f == 7 and c + 1 < NCH:
                                self.tanh(c + 1)
                    self.high_h(NCH * NF - 2)
                    self.high_h(NCH * NF - 1)
                    self.evac_y(NCH - 1)

            def evac_xTa(k, bank=SIDE_BANK):
                act.wait_ge(xTa_psum, k + 1)
                ge(act, v_psum, k)
                act.activation(xTa[:], ps[:, bank, :], ACT.Copy).then_inc(xTa_ready, 1)

            def evac_qk(k, s):
                act.wait_ge(qk_psum, 2 * k + s + 1)
                ge(act, part2_ready, k - 1)
                bias, scale = (bqs[:, 0:1], SCALE) if s == 0 else (bqk[:, 1:2], 1.0)
                act.activation(qf[k % 2][:, s, :], ps[:, SIDE_BANK, :], ACT.Identity, bias=bias, scale=scale).then_inc(qf_ready, 1)

            def evac_v(k):
                act.wait_ge(v_psum, k + 1)
                j = (k % CB) * TC
                if k == 0:
                    act.wait_ge(vpads_done, 1)
                act.activation(Vs[:, k // CB, j:j + TC, :, 0:HS],
                               ps[:, SIDE_BANK, :].rearrange("p (t h d) -> p t h d", h=H, d=HS), ACT.Copy).then_inc(v_ready, 1)

            def part0(k, s):
                act.wait_ge(qf_ready, 2 * k + s + 1)
                ge(act, parts_stored, (k - 1) * NQ * 16)
                act.activation(qp[k % 2][:, s, 0, :], qf[k % 2][:, s, :], ACT.Copy).then_inc(part0_ready, 1)

            def part1(k):
                act.wait_ge(rest_ready, k + 1)
                act.activation(qp[k % 2][:, :, 1, :], qr[k % 2], ACT.Copy).then_inc(part1_ready, 1)

            def side0(c, f):
                if f == 9 and c >= 1:
                    evac_xTa(c - 1)
                if c >= 2:
                    if f == 0:
                        evac_qk(c - 2, 0)
                    if f == 1:
                        evac_qk(c - 2, 1)
                    if f == 2:
                        evac_v(c - 2)

            def side0_after(c, f):
                if c >= 2:
                    if f == 0:
                        part0(c - 2, 0)
                    if f == 1:
                        part0(c - 2, 1)
                    if f == 3:
                        part1(c - 2)

            def evac_o(K):
                N, cc = K // 2, K % 2
                act.wait_ge(pv_done, N * NU + (TC if cc == 0 else NU))
                if K == 0:
                    act.wait_ge(parts_stored, NCH * NQ * 16)
                act.activation(oT[:, N // NQ, N % NQ, cc * CH:(cc + 1) * CH], ps[:, O_BANK, :], ACT.Copy)\
                    .then_inc(o_ready, 1)

            def evac_atT(k, bank):
                act.wait_ge(atT_psum, k + 1)
                ge(act, mo_psum, k)
                act.activation(atT[:], ps[:, bank, :], ACT.Identity, bias=bvc[:, 0:1]).then_inc(atT_ready, 1)

            def side1(c, f):
                if f == 7 and c < CB:
                    evac_atT(CB + c, SIDE_BANK)

            def high(w, src, loaded):
                act.wait_ge(loaded, 16)
                act.activation(w, src, ACT.Copy).then_inc(high_parts, 1)

            first = Ffn(ffn_sems[0])
            high(wrh[:], wr_in, wr_loaded)
            first.evac_xT(0)
            high(wgh[:], wg_in, wg_loaded)
            high(wuh[:], wu_in, wu_loaded)
            first.evac_lgT(0)
            high(wdh[:], wd_in, wd_loaded)
            first.tanh(0)
            first.silu(0, 0)
            act.wait_ge(attn_w_loaded, 8 * 16)
            act.mul(bqs[:], bqk[:, 0:1], SCALE).then_inc(bqs_ready, 1)
            act.wait_ge(bqs_ready, 1)
            first.run(side0, side0_after)
            evac_qk(NCH - 2, 0)
            part0(NCH - 2, 0)
            evac_qk(NCH - 2, 1)
            part0(NCH - 2, 1)
            evac_v(NCH - 2)
            part1(NCH - 2)
            evac_xTa(NCH - 1, FRONT_BANK)
            evac_qk(NCH - 1, 0)
            part0(NCH - 1, 0)
            evac_qk(NCH - 1, 1)
            part0(NCH - 1, 1)
            evac_v(NCH - 1)
            part1(NCH - 1)
            second = Ffn(ffn_sems[1])
            for U in range(NN * NU):
                N, u = U // NU, U % NU
                w = unit_shape(*UNITS[u])[1]
                ge(act, pv_done, U - NPB + 1)
                if N == NN - 1:
                    if u == 3:
                        evac_atT(0, PROJ_BANKS[1])
                    if u == 6:
                        second.evac_xT(0, FRONT_BANK2)
                    if u == 7:
                        evac_atT(1, PROJ_BANKS[1])
                    if u == 8:
                        second.evac_lgT(0, FRONT_BANK2)
                for h in range(HQ):
                    i = U * HQ + h
                    act.wait_ge(st_psum, i + 1)
                    act.activation(pr[:, U % NPB, h, 0:w], ps[:, st_bank(i), 0:w], ACT.Exp).then_inc(exp_done, 1)
                if u == TC:
                    evac_o(2 * N)
                if u == 0 and N:
                    evac_o(2 * N - 1)
                if N == NN - 1 and u == 9:
                    second.tanh(0)
            evac_o(2 * NN - 1)
            second.evac_cT(0, FRONT_BANK2)
            second.silu(0, 0)
            second.run(side1, lambda c, f: None, weights_out=True)

        @blk.tensor
        def _(pe):
            class Ffn:
                def __init__(self, s):
                    self.s, self.use = s, ffn_sems.index(s)

                def product(self, dst, high, low, c):
                    pe.matmul(dst, high, xTh[:, c % 2, :], start=True, stop=False)
                    pe.matmul(dst, high, xTl[:, c % 2, :], start=False, stop=False)
                    return pe.matmul(dst, low, xTh[:, c % 2, :], start=False, stop=True)

                def turn_x(self, c, bank=FRONT_BANK):
                    pe.wait_ge(self.s["xn_ready"], c + 1)
                    for t in range(TC):
                        ins = pe.transpose(ps[:, bank, t * P:(t + 1) * P], xn[:, 0, t, :], ident[:])
                    ins.then_inc(self.s["xT_psum"], 1)

                def logits(self, c, bank=FRONT_BANK):
                    pe.wait_ge(self.s["xTl_ready"], c + 1)
                    self.product(ps[0:NR, bank, :], wrh[:], wrl[:], c).then_inc(self.s["lgT_psum"], 1)

                def turn_logits(self, c, bank=FRONT_BANK):
                    pe.wait_ge(self.s["lgT_ready"], c + 1)
                    for t in range(TC):
                        ins = pe.transpose(ps[:, bank, t * NR:(t + 1) * NR], lgT[:, t * P:(t + 1) * P], ident[0:NR, 0:NR])
                    ins.then_inc(self.s["lg_psum"], 1)

                def turn_weights(self, c, bank=FRONT_BANK):
                    pe.wait_ge(self.s["cp_ready"], c + 1)
                    for t in range(TC):
                        ins = pe.transpose(ps[0:3 * NR, bank, 0:CH // 2].bitcast(BF16)[:, t * P:(t + 1) * P],
                                           cp[:, t, :, :].rearrange("p a r -> p (a r)"), identb[:])
                    ins.then_inc(self.s["cT_psum"], 1)

                def up(self, c, f, between=lambda: None):
                    s, g = self.s, c * NF + f
                    ge(pe, s["sg_ready"], g)
                    self.product(ps[:, G_BANK, :], wgh[:, f, :], wgl[:, f, :], c).then_inc(s["g_psum"], 1)
                    between()
                    ge(pe, s["su_done"], g - 1)
                    self.product(ps[:, U_BANKS[f % 2], :], wuh[:, f, :], wul[:, f, :], c).then_inc(s["u_psum"], 1)

                def weights(self, g):
                    if g < 0:
                        return
                    s, (c, f) = self.s, divmod(g, NF)
                    if f == 0:
                        pe.wait_ge(s["cT_ready"], c + 1)
                    ge(pe, s["h_ready"], g if c_bank(self.use, g) == c_bank(self.use, g - 1) else g - 1)
                    pe.matmul(ps[:, c_bank(self.use, g), :], sel[:, f, :], cT[:, c % 2, :], start=True, stop=True)\
                        .then_inc(s["c_psum"], 1)

                def down(self, g):
                    if g < 0:
                        return
                    c, f = divmod(g, NF)
                    if g == 0:
                        pe.wait_ge(wdl_ready, 1)
                    pe.wait_ge(self.s["hh_ready"], g + 1)
                    if f == 0:
                        ge(pe, self.s["yT_ready"], c)
                    y, high = ps[:, Y_BANK, :], hh[:, f % 2, :]
                    pe.matmul(y, wdh[:, f, :], high, start=f == 0, stop=False)
                    pe.matmul(y, wdl[:, f, :], high, start=False, stop=False)
                    pe.wait_ge(self.s["hl_ready"], g + 1)
                    pe.matmul(y, wdh[:, f, :], hl[:, f % 2, :], start=False, stop=f == NF - 1).then_inc(self.s["h_used"], 1)

                def turn_y(self, c, bank=SIDE_BANK):
                    pe.wait_ge(self.s["yT_ready"], c + 1)
                    for t in range(TC):
                        ins = pe.transpose(ps[:, bank, t * P:(t + 1) * P], yT[:, t * P:(t + 1) * P], ident[:])
                    ins.then_inc(self.s["yb_psum"], 1)

                def run(self, early, after, weights_turned=False):
                    for c in range(NCH):
                        for f in range(NF):
                            early(c, f, 0)
                            if f == 1 and (c or not weights_turned):
                                self.up(c, f, lambda: self.turn_weights(c))
                            elif c or f:
                                self.up(c, f)
                            early(c, f, 1)
                            self.weights(c * NF + f - 1)
                            self.down(c * NF + f - 3)
                            if c + 1 < NCH:
                                if f == 2:
                                    self.turn_x(c + 1)
                                if f == 4:
                                    self.logits(c + 1)
                                if f == 5:
                                    self.turn_logits(c + 1)
                            after(c, f)
                    self.weights(NCH * NF - 1)
                    for g in range(NCH * NF - 3, NCH * NF):
                        self.down(g)
                        after(NCH, g - NCH * NF)

            first, second = Ffn(ffn_sems[0]), Ffn(ffn_sems[1])

            def turn_xa(k, bank=SIDE_BANK):
                pe.wait_ge(xn2_ready, k + 1)
                for t in range(TC):
                    ins = pe.transpose(ps[:, bank, t * P:(t + 1) * P], xn[:, 1, t, :], ident[:])
                ins.then_inc(xTa_psum, 1)

            def project_qk(k, s):
                if s == 0:
                    pe.wait_ge(xTa_ready, k + 1)
                else:
                    pe.wait_ge(qf_ready, 2 * k + 1)
                pe.matmul(ps[:, SIDE_BANK, :], (wq, wk)[s][:], xTa[:], start=True, stop=True).then_inc(qk_psum, 1)

            def project_v(k):
                pe.wait_ge(qf_ready, 2 * k + 2)
                for t in range(TC):
                    ins = pe.matmul(ps[:, SIDE_BANK, t * P:(t + 1) * P], xTa[:, t * P:(t + 1) * P], wv[:],
                                    start=True, stop=True)
                ins.then_inc(v_psum, 1)

            def side0(c, f):
                if c == NCH:
                    if f == -3:
                        pe.wait_ge(first.s["h_ready"], NCH * NF)
                        a_turn(0, EARLY)
                        a_turn(0, EARLY + 1)
                    else:
                        a_turn(0, EARLY + 4 + f)
                    return
                if c >= 2:
                    if f == 0:
                        project_qk(c - 2, 1)
                    if f == 1:
                        project_v(c - 2)
                if c >= 1:
                    if f == 4:
                        ge(pe, v_ready, c - 1)
                        first.turn_y(c - 1)
                    if f == 8:
                        turn_xa(c - 1)
                    if f == 9:
                        project_qk(c - 1, 0)

            def a_turn(N, k):
                n, a = N % NQ, turn_no(N, k)
                if k == 0:
                    pe.wait_ge(stack_loaded[n], (4 if N == 0 else 8 if N < NQ else 17) * 16)
                    if N == 0:
                        pe.wait_ge(pads_loaded, 2 * 16)
                if N == 0 and TURNS[k] == HALF1[0]:
                    pe.wait_ge(stack_loaded[0], 8 * 16)
                bank, turn = bank_of(a), TURNS[k]
                ge(pe, a_done, turns_before(a))
                if turn == "max0" or turn == "max1":
                    if turn == "max0":
                        half, M = 0, N
                        pe.wait_ge(a_done, turn_no(N, TURNS.index(HALF0[-1])) + 1)
                    else:
                        half, M = 1, N - 1
                        pe.wait_ge(max1_ready, M + 1)
                    pe.transpose(ps[0:HQ * TC, bank, 0:P],
                                 mmx[:, M % 2, half, :, :].rearrange("p h i -> p (h i)"), ident[:]).then_inc(a_psum, 1)
                    return
                half, h, i, piece = turn
                w = CH if half > piece else (i + 1) * P
                pe.matmul(ps[:, bank, 0:w], Qs[:, n, half, h, i * P:(i + 1) * P], Ks[:, n, piece, h, 0:w],
                          start=True, stop=True).then_inc(a_psum, 1)

            def early(c, f, half):
                if ((c, f), half) in EARLY_AT:
                    a_turn(0, EARLY_AT[(c, f), half])

            def scores_t(U, h):
                N, (cc, j) = U // NU, UNITS[U % NU]
                n, i = N % NQ, U * HQ + h
                ge(pe, exp_done, i + 1 - len(ST_BANKS if i < NLAST else LAST_BANKS))
                if h == 0 and j == 0:
                    pe.wait_ge(shift_loaded[cc], (N + 1) * 2 * 16)
                w = unit_shape(cc, j)[1]
                if i == NLAST:
                    pe.wait_ge(a_done, turn_no(NN, OLD) + 1)
                pe.matmul(ps[:, st_bank(i), 0:w],
                          Ks[:, n, j // TC, h, (j % TC) * P:(j % TC + 1) * P],
                          Qs[:, n, cc, h, CH - w:CH], start=True, stop=True).then_inc(st_psum, 1)

            def pv(U):
                N, (cc, j) = U // NU, UNITS[U % NU]
                q0, w, diag = unit_shape(cc, j)
                pe.wait_ge(exp_done, (U + 1) * HQ)
                if diag:
                    pe.wait_ge(p_masked, N * TB + j + 1)
                if j == 0:
                    ge(pe, o_ready, 2 * N + cc)
                for h in range(HQ):
                    ins = pe.matmul(ps[32 * h:32 * h + VC, O_BANK, CH - w:CH], Vs[:, N // NQ, j, (N % NQ) * HQ + h, :],
                                    pr[:, U % NPB, h, 0:w], start=j == 0, stop=j == TC * (cc + 1) - 1,
                                    tile_position=(0, 32 * h))
                ins.then_inc(pv_done, 1)

            def turn_o(k, i, bank):
                for n in range(NQ):
                    t0 = (k % CB) * CH + i * P
                    ins = pe.transpose(ps[:, bank, n * P:(n + 1) * P], oT[:, k // CB, n, t0:t0 + P], ident[:])
                ins.then_inc(ot_psum, 1)

            def turn_at(k, bank):
                pe.wait_ge(at_done, (k + 1) * TC)
                for t in range(TC):
                    ins = pe.transpose(ps[:, bank, t * P:(t + 1) * P], at[:, t, :], ident[:])
                ins.then_inc(atT_psum, 1)

            def project_out(k, bank):
                pe.wait_ge(atT_ready, k + 1)
                for t in range(TC):
                    ins = pe.matmul(ps[:, bank, t * P:(t + 1) * P], atT[:, t * P:(t + 1) * P], wm[:], start=True, stop=True)
                ins.then_inc(mo_psum, 1)

            def side1(c, f):
                if c == NCH:
                    return
                k = CB + c
                if c < CB:
                    if f == 0:
                        pe.wait_ge(o_ready, 2 * NN)
                        ge(pe, xa_added, k if c else 0)
                        turn_o(k, 0, SIDE_BANK)
                        turn_o(k, 1, EXTRA_BANK)
                    if f in (2, 4):
                        pe.wait_ge(at_done, k * TC + f - 1)
                        turn_o(k, 1 + f // 2, SIDE_BANK)
                    if f == 6:
                        turn_at(k, SIDE_BANK)
                    if f == 8:
                        project_out(k, SIDE_BANK)
                if (c, f) in SECOND_Y:
                    if c == CB:
                        pe.wait_ge(xa_added, NCH)
                    ge(pe, second.s["y_added"], SECOND_Y[c, f])
                    second.turn_y(SECOND_Y[c, f])

            pe.wait_ge(ident_done, 1)
            first.turn_x(0)
            pe.wait_ge(wrl_ready, 1)
            first.logits(0)
            first.turn_logits(0)
            pe.wait_ge(low_parts, 2)
            first.up(0, 0)
            pe.wait_ge(sel_done, 1)
            pe.wait_ge(attn_w_loaded, 8 * 16)
            first.run(early, side0)

            first.turn_y(NCH - 1, FRONT_BANK)
            for k in range(EARLY + 4, NTURN):
                a_turn(0, k)
                if k == EARLY + 4:
                    project_qk(NCH - 2, 1)
                if k == EARLY + 6:
                    project_v(NCH - 2)
                if k == EARLY + 11:
                    turn_xa(NCH - 1, FRONT_BANK)
                if k == EARLY + 14:
                    pe.wait_ge(v_ready, NCH - 1)
                    project_qk(NCH - 1, 0)
                if k == EARLY + 17:
                    project_qk(NCH - 1, 1)
                if k == EARLY + 20:
                    project_v(NCH - 1)
            pe.wait_ge(v_ready, NCH)
            for U in range(NN * NU):
                N, u = U // NU, U % NU
                for h in range(HQ):
                    scores_t(U, h)
                    for k in TURNS_AT[u, h]:
                        if N + 1 < NN or k == OLD:
                            a_turn(N + 1, k)
                if U:
                    pv(U - 1)
                if N == NN - 1:
                    k = 0 if u < TC else 1
                    if u in (0, TC):
                        if k == 1:
                            pe.wait_ge(xa_added, 1)
                        for i in range(3):
                            turn_o(k, i, PROJ_BANKS[i])
                    if u in (1, TC + 1):
                        pe.wait_ge(at_done, k * TC + 1)
                        turn_o(k, 3, PROJ_BANKS[0])
                    if u in (2, TC + 2):
                        turn_at(k, PROJ_BANKS[1])
                    if u in (3, TC + 3):
                        project_out(k, PROJ_BANKS[0])
                    if u == 5:
                        pe.wait_ge(at_done, TC + 3)
                        second.turn_x(0, FRONT_BANK2)
                    if u == 7:
                        second.logits(0, FRONT_BANK2)
                    if u == 8:
                        second.turn_logits(0, FRONT_BANK2)
            pv(NN * NU - 1)
            second.turn_weights(0, FRONT_BANK2)
            pe.wait_ge(xa_added, 2)
            pe.wait_ge(o_ready, 2 * NN)
            second.up(0, 0)
            second.run(lambda c, f, half: None, side1, weights_turned=True)
            pe.wait_ge(second.s["y_added"], NCH - 1)
            second.turn_y(NCH - 1)

        @blk.vector
        def _(dve):
            steps = [0]

            def step(ins):
                steps[0] += 1
                ins.then_inc(vstep, 1)
                dve.wait_ge(vstep, steps[0])

            def statistics(k, c, ready):
                for t in range(TC):
                    ins = dve.bn_stats(st[:, k, t, :], x[:, c * TC + t, :])
                step(ins)
                for t in range(TC):
                    ins = dve.bn_aggr(mv[:, k, t, :], st[:, k, t, :])
                step(ins)
                dve.tensor_scalar(ve[:, k, :], mv[:, k, :, 1], EPS, None, ALU.add).then_inc(ready, 1)

            def normalise_x(k, c, done, xn_ready):
                dve.wait_ge(done, c + 1)
                for t in range(TC):
                    ins = dve.tensor_scalar(xn[:, k, t, :], x[:, c * TC + t, :], mv[:, k, t, 0:1], rstd[:, k, t:t + 1],
                                            ALU.subtract, ALU.mult)
                ins.then_inc(xn_ready, 1)

            class Ffn:
                def __init__(self, s):
                    self.s, self.use = s, ffn_sems.index(s)

                def stats(self, c):
                    statistics(0, c, self.s["ve_ready"])

                def norm(self, c):
                    ge(dve, self.s["xT_psum"], c)
                    normalise_x(0, c, self.s["pow_done"], self.s["xn_ready"])

                def low_xT(self, c, bank=FRONT_BANK):
                    dve.wait_ge(self.s["xTh_ready"], c + 1)
                    dve.tensor_tensor(xTl[:, c % 2, :], ps[:, bank, :], xTh[:, c % 2, :].bitcast(F32), ALU.subtract)\
                        .then_inc(self.s["xTl_ready"], 1)

                def route(self, c, bank=FRONT_BANK):
                    s = self.s
                    dve.wait_ge(s["lg_psum"], c + 1)
                    dve.tensor_copy(lg[:], ps[:, bank, 0:TC * NR].rearrange("p (t r) -> p t r", r=NR)).then_inc(s["lg_read"], 1)
                    dve.wait_ge(s["lg_read"], c + 1)
                    for t in range(TC):
                        ins = dve.max(mx8[:, t, :], lg[:, t, 0:E])
                    step(ins)
                    dve.tensor_tensor(dz[:, 0, :], mx8[:, :, 1], mx8[:, :, 0], ALU.subtract)
                    dve.tensor_copy(dz[:, 1, :], lg[:, :, E]).then_inc(s["dz_ready"], 1)

                def experts(self, c):
                    for t in range(TC):
                        ins = dve.max_index(ix8[:, t, :], mx8[:, t, :], lg[:, t, 0:E])
                    step(ins)
                    step(dve.tensor_copy(ixf[:], ix8[:, :, 0:2]))
                    numbers = iota_e[:].unsqueeze(1).broadcast_to([P, TC, E])
                    dve.tensor_tensor(e1[:], numbers, ixf[:, :, 0:1].broadcast_to([P, TC, E]), ALU.is_equal)
                    step(dve.tensor_tensor(e2[:], numbers, ixf[:, :, 1:2].broadcast_to([P, TC, E]), ALU.is_equal))

                def weigh(self, c):
                    s = self.s
                    dve.wait_ge(s["th_ready"], c + 1)
                    step(dve.tensor_scalar(rw[:, 0:2, :], th[:], 1.0, 0.25, ALU.add, ALU.mult))
                    dve.tensor_copy(cf[:, :, E], rw[:, 1, :])
                    step(dve.tensor_scalar(rw[:, 2, :], rw[:, 0, :], -1.0, 0.5, ALU.mult, ALU.add))
                    dve.tensor_tensor(e1[:], e1[:], rw[:, 2, :].unsqueeze(2).broadcast_to([P, TC, E]), ALU.mult)
                    step(dve.tensor_tensor(e2[:], e2[:], rw[:, 0, :].unsqueeze(2).broadcast_to([P, TC, E]), ALU.mult))
                    step(dve.tensor_tensor(cf[:, :, 0:E], e1[:], e2[:], ALU.add))
                    ge(dve, s["cT_psum"], c)
                    step(dve.tensor_copy(cp[:, :, 0, :], cf[:]))
                    step(dve.tensor_tensor(cr[:], cf[:], cp[:, :, 0, :], ALU.subtract))
                    step(dve.tensor_copy(cp[:, :, 1, :], cr[:]))
                    dve.tensor_tensor(cp[:, :, 2, :], cr[:], cp[:, :, 1, :], ALU.subtract).then_inc(s["cp_ready"], 1)

                def times_u(self, g):
                    s, f = self.s, g % NF
                    dve.wait_ge(s["sg_ready"], g + 1)
                    dve.wait_ge(s["u_psum"], g + 1)
                    ge(dve, s["h_ready"], g - 2)
                    dve.tensor_tensor(su[:, g % 3, :], ps[:, U_BANKS[f % 2], :], sg[:, f % 2, :], ALU.mult).then_inc(s["su_done"], 1)

                def times_c(self, g):
                    if g < 0:
                        return
                    s, f = self.s, g % NF
                    dve.wait_ge(s["su_done"], g + 1)
                    dve.wait_ge(s["c_psum"], g + 1)
                    ge(dve, s["hl_ready"], g - 1)
                    dve.tensor_tensor(hid_h[:, f % 2, :], ps[:, c_bank(self.use, g), :], su[:, g % 3, :], ALU.mult).then_inc(s["h_ready"], 1)

                def add_y(self, c, bank=SIDE_BANK):
                    dve.wait_ge(self.s["yb_psum"], c + 1)
                    dve.tensor_tensor(xs(c), ps[:, bank, :].rearrange("p (t d) -> p t d", d=D), xs(c), ALU.add)\
                        .then_inc(self.s["y_added"], 1)

                def run(self, early, after, stats_ahead=False):
                    for c in range(NCH):
                        for f in range(NF):
                            early(c, f, 0)
                            self.times_u(c * NF + f)
                            early(c, f, 1)
                            self.times_c(c * NF + f - 1)
                            if c + 1 < NCH:
                                if f == 3:
                                    self.low_xT(c + 1)
                                if f == 6:
                                    self.route(c + 1)
                                if f == 7:
                                    self.experts(c + 1)
                                if f == 8:
                                    self.weigh(c + 1)
                            after(c, f)
                            if f == 0 and c + 1 < NCH and not stats_ahead:
                                self.stats(c + 1)
                            if f == (0 if stats_ahead else 1) and c + 1 < NCH:
                                self.norm(c + 1)
                            if f == 9 and c + 2 < NCH and stats_ahead:
                                self.stats(c + 2)
                    self.times_c(NCH * NF - 1)

            first, second = Ffn(ffn_sems[0]), Ffn(ffn_sems[1])

            def stats_a(k):
                dve.wait_ge(first.s["y_added"], k + 1)
                statistics(1, k, ve2_ready)

            def norm_a(k):
                ge(dve, xTa_psum, k)
                normalise_x(1, k, pow2_done, xn2_ready)

            def rest(k):
                dve.wait_ge(part0_ready, 2 * k + 2)
                dve.tensor_tensor(qr[k % 2], qf[k % 2], qp[k % 2][:, :, 0, :], ALU.subtract).then_inc(rest_ready, 1)

            def part2(k):
                dve.wait_ge(part1_ready, k + 1)
                dve.tensor_tensor(qp[k % 2][:, :, 2, :], qr[k % 2], qp[k % 2][:, :, 1, :], ALU.subtract).then_inc(part2_ready, 1)

            def side0(c, f):
                if c >= 1:
                    if f == 5:
                        first.add_y(c - 1)
                        stats_a(c - 1)
                    if f == 7:
                        norm_a(c - 1)
                if c >= 2:
                    if f == 2:
                        rest(c - 2)
                    if f == 4:
                        part2(c - 2)

            def early(c, f, half):
                if ((c, f), half) in EARLY_AT:
                    a_turn(0, EARLY_AT[(c, f), half])

            def a_turn(N, k):
                a = turn_no(N, k)
                dve.wait_ge(a_psum, a + 1)
                bank, turn = bank_of(a), TURNS[k]
                if turn == "max0" or turn == "max1":
                    half = int(turn[3])
                    ge(dve, shift_loaded[half], (N - half) * 2 * 16)
                    step(dve.tensor_scalar(srow[:, half, 0, :], ps[0:HQ * TC, bank, 0:P], -1.0, None, ALU.mult))
                    dve.scalar_tensor_tensor(out=srow[:, half, 1, :], in0=ps[0:HQ * TC, bank, 0:P], scalar=-1.0,
                                             in1=srow[:, half, 0, :], op0=ALU.mult, op1=ALU.subtract).then_inc(a_done, 1)
                    return
                half, h, i, piece = turn
                dst = m2[:, N % 2, h, i, piece:piece + 1] if half else mmx[:, N % 2, 0, h, i:i + 1]
                if half > piece:
                    dve.reduce_max(dst, ps[:, bank, :], AX.X).then_inc(a_done, 1)
                else:
                    w = (i + 1) * P
                    dve.tensor_tensor_reduce(out=ps[:, bank, 0:w], in0=ps[:, bank, 0:w], in1=mask[:, CH - w:CH], scale=1.0,
                                             scalar=-3e38, op0=ALU.add, op1=ALU.max, accum_out=dst).then_inc(a_done, 1)
                if k == NTURN - 1:
                    dve.wait_ge(a_done, a + 1)
                    dve.tensor_tensor(mmx[:, N % 2, 1, :, :], m2[:, N % 2, :, :, 0], m2[:, N % 2, :, :, 1],
                                      ALU.max).then_inc(max1_ready, 1)

            def normalise(k, i, bank):
                dve.wait_ge(ot_psum, k * TC + i + 1)
                heads = ps[:, bank, :].rearrange("p (h v) -> p h v", v=32)
                step(dve.reciprocal(rec[:, i, :], heads[:, :, HS]))
                if i == 0:
                    ge(dve, atT_psum, k)
                dve.tensor_tensor(at[:, i, :].rearrange("p (h d) -> p h d", d=HS), heads[:, :, 0:HS],
                                  rec[:, i, :].unsqueeze(2).broadcast_to([P, H, HS]), ALU.mult).then_inc(at_done, 1)

            def add_out(k, bank):
                dve.wait_ge(mo_psum, k + 1)
                dve.tensor_tensor(xs(k), ps[:, bank, :].rearrange("p (t d) -> p t d", d=D), xs(k), ALU.add).then_inc(xa_added, 1)

            def side1(c, f):
                if c < CB:
                    if f == 1:
                        normalise(CB + c, 0, SIDE_BANK)
                        normalise(CB + c, 1, EXTRA_BANK)
                    if f in (3, 5):
                        normalise(CB + c, (f + 1) // 2, SIDE_BANK)
                    if f == 9:
                        add_out(CB + c, SIDE_BANK)
                        dve.wait_ge(xa_added, CB + c + 1)
                if (c, f - 1) in SECOND_Y:
                    second.add_y(SECOND_Y[c, f - 1])

            def low(n, w, src, high):
                dve.wait_ge(high_parts, n)
                dve.tensor_tensor(w, src, high.bitcast(F32), ALU.subtract).then_inc(low_parts, 1)

            dve.wait_ge(x_first_loaded, 16)
            first.stats(0)
            first.norm(0)
            dve.wait_ge(high_parts, 1)
            dve.tensor_tensor(wrl[:], wr_in, wrh[:].bitcast(F32), ALU.subtract).then_inc(wrl_ready, 1)
            first.low_xT(0)
            low(2, wgl[:], wg_in, wgh[:])
            low(3, wul[:], wu_in, wuh[:])
            dve.wait_ge(iota_done, 1)
            first.route(0)
            first.experts(0)
            first.weigh(0)
            dve.wait_ge(x_rest_loaded, 16)
            dve.wait_ge(attn_w_loaded, 8 * 16)
            first.run(early, side0)
            for k in range(EARLY, NTURN):
                a_turn(0, k)
                if k == EARLY + 4:
                    first.add_y(NCH - 1, FRONT_BANK)
                    stats_a(NCH - 1)
                if k == EARLY + 8:
                    norm_a(NCH - 1)
            for N in range(1, NN):
                for k in range(NTURN):
                    a_turn(N, k)
            a_turn(NN, OLD)
            for c in range(NCH):
                ins = dve.tensor_tensor(xs(c), xs(c), bmb[:].unsqueeze(1).broadcast_to([P, TC, D]), ALU.add)
            step(ins)
            for i in range(TC):
                normalise(0, i, PROJ_BANKS[i % 3])
            add_out(0, PROJ_BANKS[0])
            dve.wait_ge(xa_added, 1)
            second.stats(0)
            normalise(1, 0, PROJ_BANKS[0])
            second.norm(0)
            for i in range(1, TC):
                normalise(1, i, PROJ_BANKS[i % 3])
            second.low_xT(0, FRONT_BANK2)
            add_out(1, PROJ_BANKS[0])
            second.route(0, FRONT_BANK2)
            second.experts(0)
            second.weigh(0)
            dve.wait_ge(xa_added, 2)
            second.stats(1)
            second.run(lambda c, f, half: None, side1, stats_ahead=True)
            second.add_y(NCH - 1)


_OUT = ("out_dram", (B, S, D))


def kernel(**inputs):
    import numpy as np
    import concourse.bacc as bacc
    from concourse.bass_utils import run_bass_kernel_spmd

    a = {k.removeprefix("L0_"): np.asarray(v) for k, v in inputs.items()}
    hid = lambda e, s: np.concatenate([e.reshape(E * MH, D), s], 0).T
    arrays = {
        "x": a["attn_x"].reshape(T, D),
        "w_gate": hid(a["ffn_We_gate"], a["ffn_Ws_gate"]),
        "w_up": hid(a["ffn_We_up"], a["ffn_Ws_up"]),
        "w_down": np.concatenate([a["ffn_We_down"].transpose(0, 2, 1).reshape(E * MH, D), a["ffn_Ws_down"].T], 0),
        "w_route": np.concatenate([a["ffn_Wg"], a["ffn_Wsg"]], 0).T,
    }
    for n in ("Wq", "bq", "Wk", "bk"):
        w = a["attn_" + n]
        arrays[n] = w.reshape(w.shape[:-1] + (NQ, HQ, HS)).swapaxes(-1, -2).reshape(w.shape)
    for n in ("Wv", "bv", "Wm", "bm"):
        arrays[n] = a["attn_" + n]
    arrays = {f"in_{n}": np.ascontiguousarray(v) for n, v in arrays.items()}
    nc = bacc.Bacc("TRN2", target_bir_lowering=False, num_devices=1)
    args = [nc.dram_tensor(n, v.shape, mybir.dt.from_np(v.dtype), kind="ExternalInput").ap() for n, v in arrays.items()]
    args.append(nc.dram_tensor(_OUT[0], (T, D), F32, kind="ExternalOutput").ap())
    macaron(nc, *args)
    r = run_bass_kernel_spmd(nc, [arrays], core_ids=[0])
    return r.results[0][_OUT[0]].reshape(_OUT[1])
```
